# Optimizing a Trainium2 kernel written in Bass

```python
import numpy as np
import jax
import jax.numpy as jnp

def _softmax(x, axis=-1):
    return jax.nn.softmax(x, axis=axis)

def _gelu(x):
    return jax.nn.gelu(x, approximate=True)

def _silu(x):
    return jax.nn.silu(x)

def _sigmoid(x):
    return jax.nn.sigmoid(x)

def _layernorm(x, axis=-1, eps=1e-05):
    m = jnp.mean(x, axis=axis, keepdims=True)
    v = jnp.var(x, axis=axis, keepdims=True)
    return (x - m) / jnp.sqrt(v + eps)

def _scatter_add(tgt, idx, src, axis=0):
    return tgt.at[idx].add(src)

def _segment_sum(src, seg, n):
    return jax.ops.segment_sum(src, seg, n)
kernel_name = 'mk_seq_preln_d1_jaxref_r4_aad26a'

def setup_inputs(seed: int=0):
    np.random.seed(seed)
    _w = jnp.asarray

    def _L0_attn_setup():
        import jax, jax.numpy as jnp
        import numpy as np
        N_HEADS = 16
        CHUNK = 128

        def _phi(x):
            return jax.nn.elu(x) + 1.0
        key = jax.random.key(seed)
        ks = jax.random.split(key, 5)
        d = 256
        scale = (2.0 / (d + d)) ** 0.5
        W = lambda k: jax.random.normal(k, (d, d), jnp.float32) * scale
        return {'x': jax.random.normal(ks[0], (4, 1024, d), jnp.float32), 'Wq': W(ks[1]), 'bq': jnp.zeros((d,), jnp.float32), 'Wk': W(ks[2]), 'bk': jnp.zeros((d,), jnp.float32), 'Wv': W(ks[3]), 'bv': jnp.zeros((d,), jnp.float32), 'Wo': W(ks[4]), 'bo': jnp.zeros((d,), jnp.float32)}
    _L0_attn_in = _L0_attn_setup()

    def _L0_ffn_setup():
        import jax, jax.numpy as jnp
        import numpy as np
        B, S, H, F, G = (8, 512, 256, 1024, 128)
        EPS = 1e-05

        def _dequant(q, scales, g):
            K, N = q.shape
            w = (q.astype(jnp.float32) - 128.0).reshape(K // g, g, N) * scales[:, None, :]
            return w.reshape(K, N)
        key = jax.random.key(seed)
        ks = jax.random.split(key, 8)
        x = jax.random.normal(ks[0], (B, S, H), dtype=jnp.float32)
        ln_gamma = jnp.ones((H,), jnp.float32)
        ln_beta = jnp.zeros((H,), jnp.float32)
        fc1_q = jax.random.randint(ks[1], (H, F), 0, 64, dtype=jnp.int32)
        fc2_q = jax.random.randint(ks[2], (F, H), 0, 64, dtype=jnp.int32)
        fc1_scales = jax.random.uniform(ks[3], (H // G, F), jnp.float32) * 0.02 + 0.001
        fc2_scales = jax.random.uniform(ks[4], (F // G, H), jnp.float32) * 0.02 + 0.001
        fc1_bias = jax.random.normal(ks[5], (F,), jnp.float32) * 0.02
        fc2_bias = jax.random.normal(ks[6], (H,), jnp.float32) * 0.02
        return {'x': x, 'ln_gamma': ln_gamma, 'ln_beta': ln_beta, 'fc1_q': fc1_q, 'fc1_scales': fc1_scales, 'fc1_bias': fc1_bias, 'fc2_q': fc2_q, 'fc2_scales': fc2_scales, 'fc2_bias': fc2_bias}
    _L0_ffn_in = _L0_ffn_setup()
    _d = {'L0_attn_x': _L0_attn_in['x'], 'L0_attn_Wq': _L0_attn_in['Wq'], 'L0_attn_bq': _L0_attn_in['bq'], 'L0_attn_Wk': _L0_attn_in['Wk'], 'L0_attn_bk': _L0_attn_in['bk'], 'L0_attn_Wv': _L0_attn_in['Wv'], 'L0_attn_bv': _L0_attn_in['bv'], 'L0_attn_Wo': _L0_attn_in['Wo'], 'L0_attn_bo': _L0_attn_in['bo'], 'L0_ffn_ln_gamma': _L0_ffn_in['ln_gamma'], 'L0_ffn_ln_beta': _L0_ffn_in['ln_beta'], 'L0_ffn_fc1_q': _L0_ffn_in['fc1_q'], 'L0_ffn_fc1_scales': _L0_ffn_in['fc1_scales'], 'L0_ffn_fc1_bias': _L0_ffn_in['fc1_bias'], 'L0_ffn_fc2_q': _L0_ffn_in['fc2_q'], 'L0_ffn_fc2_scales': _L0_ffn_in['fc2_scales'], 'L0_ffn_fc2_bias': _L0_ffn_in['fc2_bias']}
    _x0 = _d['L0_attn_x']
    _d['L0_attn_x'] = jax.random.normal(jax.random.fold_in(jax.random.key(seed), 1), (32, 512, 256), dtype=_x0.dtype)
    del _x0
    return _d

def reference(L0_attn_x, L0_attn_Wq, L0_attn_bq, L0_attn_Wk, L0_attn_bk, L0_attn_Wv, L0_attn_bv, L0_attn_Wo, L0_attn_bo, L0_ffn_ln_gamma, L0_ffn_ln_beta, L0_ffn_fc1_q, L0_ffn_fc1_scales, L0_ffn_fc1_bias, L0_ffn_fc2_q, L0_ffn_fc2_scales, L0_ffn_fc2_bias):

    def _L0_attn_ref(x, Wq, bq, Wk, bk, Wv, bv, Wo, bo):
        import jax, jax.numpy as jnp
        import numpy as np
        N_HEADS = 16
        CHUNK = 128

        def _phi(x):
            return jax.nn.elu(x) + 1.0
        b, s, dm = x.shape
        h = N_HEADS
        d = dm // h

        def proj(W, bias):
            y = x @ W.T + bias
            return y.reshape(b, s, h, d).transpose(0, 2, 1, 3).reshape(b * h, s, d)
        q = _phi(proj(Wq, bq))
        k = _phi(proj(Wk, bk))
        v = proj(Wv, bv)
        C = CHUNK
        n = s // C
        to_chunks = lambda t: t.reshape(b * h, n, C, d).transpose(1, 0, 2, 3)
        qc, kc, vc = (to_chunks(q), to_chunks(k), to_chunks(v))
        mask = jnp.tril(jnp.ones((C, C), bool))

        def step(carry, inp):
            S, z = carry
            qi, ki, vi = inp
            scores = jnp.einsum('bqd,bkd->bqk', qi, ki)
            scores = jnp.where(mask, scores, jnp.zeros((), scores.dtype))
            num = jnp.einsum('bqk,bkd->bqd', scores, vi) + jnp.einsum('bqd,bde->bqe', qi, S)
            kcum = jnp.cumsum(ki, axis=1) + z[:, None, :]
            den = jnp.sum(qi * kcum, axis=-1, keepdims=True)
            out = num / den
            S2 = S + jnp.einsum('bkd,bke->bde', ki, vi)
            z2 = z + ki.sum(axis=1)
            return ((S2, z2), out)
        init = (jnp.zeros((b * h, d, d), x.dtype), jnp.zeros((b * h, d), x.dtype))
        _, outs = jax.lax.scan(step, init, (qc, kc, vc))
        out = outs.transpose(1, 0, 2, 3).reshape(b, h, s, d).transpose(0, 2, 1, 3).reshape(b, s, dm)
        return out @ Wo.T + bo

    def _L0_ffn_ref(x, ln_gamma, ln_beta, fc1_q, fc1_scales, fc1_bias, fc2_q, fc2_scales, fc2_bias):
        import jax, jax.numpy as jnp
        import numpy as np
        B, S, H, F, G = (8, 512, 256, 1024, 128)
        EPS = 1e-05

        def _dequant(q, scales, g):
            K, N = q.shape
            w = (q.astype(jnp.float32) - 128.0).reshape(K // g, g, N) * scales[:, None, :]
            return w.reshape(K, N)
        residual = x
        mu = jnp.mean(x, axis=-1, keepdims=True)
        var = jnp.mean(jnp.square(x - mu), axis=-1, keepdims=True)
        h = (x - mu) * jax.lax.rsqrt(var + EPS) * ln_gamma + ln_beta
        hf = h.reshape(-1, H)
        w1 = _dequant(fc1_q, fc1_scales, G)
        y = hf @ w1 + fc1_bias
        y = jax.nn.silu(y)
        w2 = _dequant(fc2_q, fc2_scales, G)
        z = y @ w2 + fc2_bias
        return residual + 0.5 * z.reshape(residual.shape)
    x = L0_attn_x
    x = x + _L0_attn_ref(_layernorm(x, axis=-1), L0_attn_Wq, L0_attn_bq, L0_attn_Wk, L0_attn_bk, L0_attn_Wv, L0_attn_bv, L0_attn_Wo, L0_attn_bo)
    x = x + _L0_ffn_ref(_layernorm(x, axis=-1), L0_ffn_ln_gamma, L0_ffn_ln_beta, L0_ffn_fc1_q, L0_ffn_fc1_scales, L0_ffn_fc1_bias, L0_ffn_fc2_q, L0_ffn_fc2_scales, L0_ffn_fc2_bias)
    return x

_drawn_inputs = setup_inputs


def setup_inputs(seed=0):
    import zlib

    import numpy as np

    out = dict(_drawn_inputs(seed))
    spreads = {'L0_attn_bq': (0.0, 0.8),
     'L0_attn_bk': (0.0, 0.8),
     'L0_attn_bv': (0.0, 0.1),
     'L0_attn_bo': (0.0, 0.1),
     'L0_ffn_ln_gamma': (1.0, 0.2),
     'L0_ffn_ln_beta': (0.0, 0.1)}
    factors = {'L0_attn_Wq': 7.211, 'L0_attn_Wk': 3.922, 'L0_ffn_fc1_bias': 8.0, 'L0_ffn_fc2_bias': 8.0}
    for name, (base, spread) in spreads.items():
        noise = np.random.default_rng([zlib.crc32(name.encode()), seed]).standard_normal(out[name].shape)
        drawn = base * np.exp(spread * noise) if base else spread * noise
        out[name] = jnp.asarray(drawn.astype(out[name].dtype))
    for name, factor in factors.items():
        out[name] = (out[name] * factor).astype(out[name].dtype)
    return out
```

```python
from contextlib import ExitStack

import concourse.bass as bass
from concourse import mybir
import numpy as np

F32 = mybir.dt.float32
F32R = mybir.dt.float32r
I32 = mybir.dt.int32
ALU = mybir.AluOpType
ACT = mybir.ActivationFunctionType

P = 128
EPS = 1e-5


class Event:

    def __init__(self, sem, per, step=1, early=0):
        self.sem, self.per, self.step, self.early = sem, per, step, early

    def done(self, instruction):
        return instruction.then_inc(self.sem, self.step)

    def value(self, batch, k):
        return (batch + self.early) * (self.per * self.step) + (k + 1) * self.step


class Waiter:

    def __init__(self, engine, i):
        self.engine, self.i, self.known = engine, i, {}

    def alone(self, event, shift=0, k=None):
        self.need(event, shift, k)
        self.engine.sem_inc(self.idle, 1)

    def need(self, event, shift=0, k=None):
        k = event.per - 1 if k is None else k
        if self.known.get((id(event), shift), -1) >= k:
            return
        self.known[(id(event), shift)] = k
        value = event.value(self.i + shift, k)
        if not isinstance(value, int) or value > 0:
            self.engine.wait_ge(event.sem, value)


def build(nc, x, wq_t, bq, wk_t, bk, wv_t, bv, wo_t, bo, gamma, beta, q1, sc1, b1, q2, sc2, b2, out):
    B, S, D = x.shape
    F = q1.shape[1]
    HEADS = 16
    HD = D // HEADS
    C = S // P
    T = D // P
    HT = HEADS // T
    FT = F // P
    HALF = P // 2
    U = C * T
    G1, G2 = sc1.shape[0], sc2.shape[0]
    assert D == 2 * P and S == 4 * P and HD == 16 and G1 == T and G2 == FT

    x_v = x.rearrange("b (c p) d -> b p c d", p=P)
    out_v = out.rearrange("b (c p) d -> b p c d", p=P)

    with ExitStack() as ctx:
        def sb(name, shape, dtype=F32):
            return ctx.enter_context(nc.sbuf_tensor(name, shape, dtype))

        def bank(name):
            return ctx.enter_context(nc.psum_tensor(name, [P, 512], F32))

        def sem(name):
            return ctx.enter_context(nc.semaphore(name))

        w_hi = {n: sb(f"w{n}_hi", [P, T, D], F32R) for n in "qkvo"}
        w_lo = {n: sb(f"w{n}_lo", [P, T, D], F32R) for n in "qkvo"}
        w1_hi, w1_lo = sb("w1_hi", [P, T, F], F32R), sb("w1_lo", [P, T, F], F32R)
        w2_hi, w2_lo = sb("w2_hi", [P, FT, D], F32R), sb("w2_lo", [P, FT, D], F32R)
        ident = sb("ident", [P, P])
        head_ones = sb("head_ones", [P, P])
        state_mask = sb("state_mask", [P, T, P])
        causal = sb("causal", [P, 2, HALF])
        head_col = sb("head_col", [P, HT])
        ones = sb("ones", [P, 1])
        minus_half = sb("minus_half", [P, C])
        bias_qk = sb("bias_qk", [P, 2, T])
        bias_qkm = sb("bias_qkm", [P, 2, T])
        bias_qk1 = sb("bias_qk1", [P, 2, T])
        bias_1 = sb("bias_1", [P, FT])
        bias_1in = sb("bias_1in", [P, FT])
        gamma_c, beta_c, bv_c = sb("gamma_c", [P, T]), sb("beta_c", [P, T]), sb("bv_c", [P, T])
        bias_o = sb("bias_o", [P, D])
        bias_2 = sb("bias_2", [P, D])

        x_in = sb("x_in", [P, C, D])
        xb = sb("xb", [P, C, D])
        x_hat = sb("x_hat", [P, C, D])
        xt_hi, xt_lo = sb("xt_hi", [P, T, S], F32R), sb("xt_lo", [P, T, S], F32R)
        clip = sb("clip", [P, 2, S])
        phi_q, phi_k = sb("phi_q", [P, T, S]), sb("phi_k", [P, T, S])
        qk = sb("qk", [P, T, S])
        q_heads = sb("q_heads", [P, T, HT, S])
        k_tok = sb("k_tok", [P, C, D])
        v_pad = sb("v_pad", [P, C, HT * T // 2, 4, HD])
        probs = [sb(f"probs{n}", [P, HT, P]) for n in range(2)]
        state = sb("state", [P, 2, T, P])
        gt_hi, gt_lo = sb("gt_hi", [P, T, S], F32R), sb("gt_lo", [P, T, S], F32R)
        x1 = sb("x1", [P, C, D])
        hn = sb("hn", [P, C, D])
        hn2 = sb("hn2", [P, C, D])
        res = sb("res", [P, C, D])
        silu_f = sb("silu_f", [P, 2, S])
        s_hi, s_lo = sb("s_hi", [P, FT, S], F32R), sb("s_lo", [P, FT, S], F32R)
        stats1, stats2 = sb("stats1", [P, C, 6]), sb("stats2", [P, C, 6])
        mv1, mv2 = sb("mv1", [P, C, 2]), sb("mv2", [P, C, 2])
        ve1, rstd1 = sb("ve1", [P, C]), sb("rstd1", [P, C])
        tiny = sb("tiny", [P, 6, C])
        stage_qkvo = {n: t for n, t in zip("qkvo", (phi_q, phi_k, k_tok, x1))}
        stage = q_heads[:, :, :, :].rearrange("p t h s -> p (t h s)")
        N1, N2 = T * F, FT * D
        q1_i = stage[:, 0:N1].bitcast(I32).rearrange("p (g n) -> p g n", g=T)
        sc1_b = stage[:, N1:2 * N1].rearrange("p (g n) -> p g n", g=T)
        q2_i = stage[:, 2 * N1:2 * N1 + N2].bitcast(I32).rearrange("p (g n) -> p g n", g=FT)
        sc2_b = stage[:, 2 * N1 + N2:2 * (N1 + N2)].rearrange("p (g n) -> p g n", g=FT)
        w1_f = stage[:, 0:N1].rearrange("p (g n) -> p g n", g=T)
        w2_f = stage[:, 2 * N1:2 * N1 + N2].rearrange("p (g n) -> p g n", g=FT)

        num = [bank(f"num{t}") for t in range(T)]
        state_acc = bank("state_acc")
        sc_a, sc_b = bank("sc_a"), bank("sc_b")
        ring = [bank(f"ring{n}") for n in range(3)]
        USES = (["k0", "q0", "k1", "q1", "v0", "v1", "ht0", "ht1", "f0", "f1", "kt0", "kt1", "f2",
                 "den0", "f3", "den1", "f4", "f5", "f6", "f7", "z0", "wo0", "wo1", "xt0", "xt1", "z1"])
        FFN_USES = {"ht0", "ht1", "z0", "z1"} | {f"f{j}" for j in range(FT)}

        def ring_bank(use):
            return ring[USES.index(use) % 3]

        def ev(name, per, **more):
            return Event(sem(name), per, **more)

        load = ev("load", 1, step=16)
        ln1_st = ev("ln1_st", 1)
        ln1_mv = ev("ln1_mv", 1)
        ln1_ve = ev("ln1_ve", 1)
        ln1_r = ev("ln1_r", 1)
        xhat = ev("xhat", 1)
        e_xb = ev("e_xb", 1)
        xt_pe, xt_h, xt_l = ev("xt_pe", T), ev("xt_h", T), ev("xt_l", T)
        qk_pe, qk_exp, qk_clip, phi = ev("qk_pe", 2 * T), ev("qk_exp", 2 * T), ev("qk_clip", 2 * T), ev("phi", 2 * T)
        v_pe, v_sb = ev("v_pe", C // 2), ev("v_sb", C)
        kt_pe, kt_sb = ev("kt_pe", C // 2), ev("kt_sb", C // 2)
        kcum, qkcum = ev("kcum", T), ev("qkcum", T)
        qh0, qh1 = ev("qh0", 1), ev("qh1", 1)
        sc_pe, masked = ev("sc_pe", U), ev("masked", 2 * U)
        upd_pe, snap = ev("upd_pe", C - 1), ev("snap", C - 1)
        av_pe = ev("av_pe", U)
        den_pe, den_sb, rden = ev("den_pe", T), ev("den_sb", T), ev("rden", U)
        attn, at_h, at_l = ev("attn", T), ev("at_h", T), ev("at_l", T)
        wo_pe, e_x1 = ev("wo_pe", C // 2), ev("e_x1", C // 2)
        ln2_v = ev("ln2_v", 6)
        ln2_p = ev("ln2_p", 2)
        e_hn, e_hn2 = ev("e_hn", 1), ev("e_hn2", 1)
        res_a, e_res = ev("res_a", 1), ev("e_res", 1)
        F_ = dict(early=1)
        ht_pe, ht_h, ht_l = ev("ht_pe", T, **F_), ev("ht_h", T, **F_), ev("ht_l", T, **F_)
        f_pe, silu, sh, sl = ev("f_pe", FT, **F_), ev("silu", FT, **F_), ev("sh", FT, **F_), ev("sl", FT, **F_)
        z_pe, e_out = ev("z_pe", C // 2, **F_), ev("e_out", C // 2, **F_)
        store = ev("store", 1, step=16, **F_)

        Waiter.idle = sem("idle")
        p_const, p_dma, p_wdma = sem("p_const"), sem("p_dma"), [sem(f"p_wdma{n}") for n in range(3)]
        p_split_a, p_split_v, p_v, p_pe, p_a = sem("p_split_a"), sem("p_split_v"), sem("p_v"), sem("p_pe"), sem("p_a")

        LAST_READ = {
            "k0": (phi, 0), "q0": (phi, 1), "k1": (phi, 2), "q1": (phi, 3), "v0": (v_sb, 1), "v1": (v_sb, 3),
            "ht0": (ht_l, 0), "ht1": (ht_l, 1), "kt0": (kt_sb, 0), "kt1": (kt_sb, 1), "den0": (den_sb, 0),
            "den1": (den_sb, 1), "z0": (e_out, 0), "z1": (e_out, 1), "wo0": (e_x1, 0), "wo1": (e_x1, 1),
            "xt0": (xt_l, 0), "xt1": (xt_l, 1),
        } | {f"f{j}": (silu, j) for j in range(FT)}

        def batch_shift(use):
            return -1 if use in FFN_USES else 1 if use in ("xt0", "xt1") else 0

        def free_bank(w, use, present):
            n = USES.index(use)
            m = n - 1
            while True:
                earlier = m < 0
                other = USES[m % len(USES)]
                shift = batch_shift(other) - earlier
                exists = other in present or (earlier and not (isinstance(w.i, int) and w.i + shift >= B))
                if USES.index(other) % 3 == USES.index(use) % 3 and exists:
                    event, k = LAST_READ[other]
                    w.need(event, shift, k)
                    return
                m -= 1

        def pe_split3(e, target, pairs):
            n = 0
            for (lh, ll), (rh, rl) in pairs:
                for a, b in ((lh, rh), (lh, rl), (ll, rh)):
                    last = e.matmul(target, a, b, start=(n == 0), stop=(n == 3 * len(pairs) - 1))
                    n += 1
            return last

        def pe_projection(e, w, n, m, use, present):
            free_bank(w, use, present)
            cols = slice(m * P, (m + 1) * P)
            last = pe_split3(e, ring_bank(use)[:, :], [
                ((w_hi[n][:, t, cols], w_lo[n][:, t, cols]), (xt_hi[:, t, :], xt_lo[:, t, :])) for t in range(T)])
            qk_pe.done(last)

        def pe_tokens(e, w, n, lhs, use, present, event):
            free_bank(w, use, present)
            for h in range(2):
                toks = slice((2 * int(use[-1]) + h) * P, (2 * int(use[-1]) + h + 1) * P)
                last = pe_split3(e, ring_bank(use)[:, h * D:(h + 1) * D], [
                    ((lhs[0][:, t, toks], lhs[1][:, t, toks]), (w_hi[n][:, t, :], w_lo[n][:, t, :])) for t in range(T)])
            event.done(last)

        def pe_transposes(e, w, src, t, use, present, event):
            free_bank(w, use, present)
            for c in range(C):
                last = e.transpose(ring_bank(use)[:, c * P:(c + 1) * P], src[:, c, t * P:(t + 1) * P], ident[:, :])
            event.done(last)

        def pe_iteration(e, i, A, Fn, N):
            w = Waiter(e, i)
            present = {u for u in USES if (Fn if u in FFN_USES else N if u in ("xt0", "xt1") else A)}

            def x_transposes():
                w.need(xhat, 1)
                for t in range(T):
                    pe_transposes(e, w, x_hat, t, f"xt{t}", present, xt_pe)

            def ffn_in():
                w.need(e_hn2, -1)
                for t in range(T):
                    pe_transposes(e, w, hn2, t, f"ht{t}", present, ht_pe)

            def fc1(j):
                if not Fn:
                    return
                w.need(ht_l, -1)
                free_bank(w, f"f{j}", present)
                cols = slice(j * P, (j + 1) * P)
                f_pe.done(pe_split3(e, ring_bank(f"f{j}")[:, :], [
                    ((w1_hi[:, t, cols], w1_lo[:, t, cols]), (gt_hi[:, t, :], gt_lo[:, t, :])) for t in range(T)]))

            def fc2(n):
                if not Fn:
                    return
                w.need(sh, -1)
                w.need(sl, -1)
                free_bank(w, f"z{n}", present)
                for h in range(2):
                    toks = slice((2 * n + h) * P, (2 * n + h + 1) * P)
                    last = pe_split3(e, ring_bank(f"z{n}")[:, h * D:(h + 1) * D], [
                        ((s_hi[:, j, toks], s_lo[:, j, toks]), (w2_hi[:, j, :], w2_lo[:, j, :])) for j in range(FT)])
                z_pe.done(last)

            def k_transposes(n):
                w.need(phi, 0, 2)
                free_bank(w, f"kt{n}", present)
                for h in range(2):
                    for t in range(T):
                        c = 2 * n + h
                        last = e.transpose(ring_bank(f"kt{n}")[:, (h * T + t) * P:(h * T + t + 1) * P],
                                           phi_k[:, t, c * P:(c + 1) * P], ident[:, :])
                kt_pe.done(last)

            def scores(u):
                c, t = divmod(u, T)
                w.need((qh0, qh1)[t])
                w.need(masked, *((0, 2 * u - 1) if u else (-1, 2 * U - 1)))
                lo, hi = slice(c * P, c * P + HALF), slice(c * P + HALF, (c + 1) * P)
                k_lo, k_hi = phi_k[:, t, lo], phi_k[:, t, hi]
                e.matmul(sc_a[0:HALF, :], k_lo, q_heads[:, t, :, lo], start=True, stop=True)
                e.matmul(sc_b[HALF:P, :], k_hi, q_heads[:, t, :, hi], start=True, stop=True)
                sc_pe.done(e.matmul(sc_b[0:HALF, :], k_lo, q_heads[:, t, :, hi], start=True, stop=True))

            def from_state(u):
                c, t = divmod(u, T)
                if c:
                    w.need(snap, 0, c - 1)
                    e.matmul(num[t][:, c * P:(c + 1) * P], state[:, (c - 1) % 2, t, :], phi_q[:, t, c * P:(c + 1) * P],
                             start=False, stop=False, skip_group_check=True)

            def update_state(c):
                w.need(kt_sb, 0, c // 2)
                w.need(v_sb, 0, c)
                if c:
                    w.need(snap, 0, c - 1)
                else:
                    w.need(snap, -1)
                for t in range(T):
                    last = e.matmul(state_acc[:, t * P:(t + 1) * P], k_tok[:, c, t * P:(t + 1) * P],
                                    v_pad[:, c, t * HT // 2:(t + 1) * HT // 2, 0:4:3, :],
                                    start=(c == 0 and t == 0), stop=True, skip_group_check=True)
                upd_pe.done(last)

            def values(u):
                c, t = divmod(u, T)
                w.need(masked, 0, 2 * u + 1)
                w.need(v_sb, 0, c)
                if c == 0:
                    w.need(attn, -1)
                for odd in range(2):
                    for pair in range(HT // 2):
                        last = e.matmul(
                            num[t][32 * pair:32 * pair + 32, c * P:(c + 1) * P],
                            v_pad[:, c, t * HT // 2 + pair, 2 * odd:2 * odd + 2, :],
                            probs[u % 2][:, 2 * pair + odd, :],
                            start=(c == 0 and odd == 0), stop=(odd == 1), skip_group_check=True)
                av_pe.done(last)

            def denominator(t):
                w.need(qkcum, 0, t)
                free_bank(w, f"den{t}", present)
                den_pe.done(e.matmul(ring_bank(f"den{t}")[:, :], head_ones[:, :], qk[:, t, :], start=True, stop=True))

            if A:
                w.need(xt_l)
                for m in range(T):
                    pe_projection(e, w, "k", m, f"k{m}", present)
                    pe_projection(e, w, "q", m, f"q{m}", present)
                for n in range(2):
                    pe_tokens(e, w, "v", (xt_hi, xt_lo), f"v{n}", present, v_pe)
            if Fn:
                ffn_in()
            fc1(0)
            fc1(1)
            if A:
                k_transposes(0)
                k_transposes(1)
            fc1(2)
            if A:
                update_state(0)
                scores(0)
                denominator(0)
            fc1(3)
            if A:
                scores(1)
                values(0)
                denominator(1)
            for u in range(2, U):
                if u < 6:
                    fc1(u + 2)
                if A:
                    if u % T == 0 and u // T < C - 1:
                        update_state(u // T)
                    scores(u)
                    from_state(u - 1)
                    values(u - 1)
            if A:
                from_state(U - 1)
                values(U - 1)
            fc2(0)
            if A:
                w.need(at_l)
                for n in range(2):
                    pe_tokens(e, w, "o", (gt_hi, gt_lo), f"wo{n}", present, wo_pe)
            if N:
                x_transposes()
            fc2(1)

        def ve_norm_x(e, w, s):
            w.need(load, s)
            for c in range(C):
                last = e.bn_stats(stats1[:, c, :], x_in[:, c, :])
            ln1_st.done(last)
            w.alone(ln1_st, s)
            for c in range(C):
                last = e.bn_aggr(mv1[:, c, :], stats1[:, c, :])
            ln1_mv.done(last)
            w.need(ln1_mv, s)
            ln1_ve.done(e.tensor_scalar(ve1[:, :], mv1[:, :, 1], EPS, None, ALU.add))

        def ve_x_hat(e, w, s):
            w.need(ln1_r, s)
            w.need(xt_pe, s - 1)
            for c in range(C):
                last = e.tensor_scalar(x_hat[:, c, :], x_in[:, c, :], mv1[:, c, 0:1], rstd1[:, c:c + 1],
                                       ALU.subtract, ALU.mult)
            xhat.done(last)

        def ve_lo(e, w, bank_, hi, lo, t, hi_event, shift, event):
            w.need(hi_event, shift, t)
            event.done(e.tensor_tensor(lo[:, t, :], bank_, hi[:, t, :].bitcast(F32), ALU.subtract))

        def ve_iteration(e, i, A, Fn, N):
            w = Waiter(e, i)

            def features(n):
                m, is_q = n // 2, n % 2
                w.need(qk_exp, 0, n)
                if is_q:
                    w.need(av_pe, -1)
                else:
                    w.need(sc_pe, -1)
                    w.need(upd_pe, -1)
                dst = phi_q if is_q else phi_k
                phi.done(e.scalar_tensor_tensor(
                    out=dst[:, m, :], in0=ring_bank("kq"[is_q] + str(m))[:, :], scalar=bias_qk1[:, 1 - is_q, m:m + 1],
                    in1=clip[:, n % 2, :], op0=ALU.add, op1=ALU.max))

            def cumulate(t):
                w.need(phi, 0, 2 * t)
                w.need(attn, -1)
                kcum.done(e.tensor_tensor_scan(qk[:, t, :], ones[:, 0:1].to_broadcast([P, S]), phi_k[:, t, :], 0.0,
                                               ALU.mult, ALU.add))

            def ffn_lo(j):
                if not Fn:
                    return
                w.need(sh, -1, j)
                w.need(z_pe, -2)
                sl.done(e.tensor_tensor(s_lo[:, j, :], silu_f[:, j % 2, :], s_hi[:, j, :].bitcast(F32), ALU.subtract))

            def mask(u):
                w.need(sc_pe, 0, u)
                if u >= 2:
                    w.need(av_pe, 0, u - 2)
                else:
                    w.need(av_pe, -1)
                pr = probs[u % 2]
                for bank_, rows, qs, m in ((sc_a, HALF, slice(0, HALF), 0), (sc_b, P, slice(HALF, P), 1)):
                    masked.done(e.tensor_tensor(
                        pr[0:rows, :, qs], bank_[0:rows, :].rearrange("p (h q) -> p h q", h=HT),
                        causal[0:rows, m, None, :].to_broadcast([rows, HT, HALF]), ALU.mult))

            def snapshot(c):
                w.need(upd_pe, 0, c)
                if c >= 2:
                    w.need(av_pe, 0, T * c - 1)
                else:
                    w.need(av_pe, -1)
                snap.done(e.tensor_tensor(state[:, c % 2, :, :], state_acc[:, 0:T * P].rearrange("p (t f) -> p t f", t=T),
                                          state_mask[:, :, :], ALU.mult))

            def reciprocals(t, n):
                w.need(den_sb, 0, t)
                part = qk[:, t, n * P:(n + 1) * P]
                rden.done(e.reciprocal(part, part))

            def final(n):
                w.need(z_pe, -1, n)
                w.need(e_res, -1)
                cs = slice(2 * n, 2 * n + 2)
                e_out.done(e.scalar_tensor_tensor(
                    out=res[:, cs, :], in0=ring_bank(f"z{n}")[:, :].rearrange("p (c d) -> p c d", c=2), scalar=0.5,
                    in1=res[:, cs, :], op0=ALU.mult, op1=ALU.add))

            if A:
                for n in range(4):
                    features(n)
            if Fn:
                for t in range(T):
                    ve_lo(e, w, ring_bank(f"ht{t}")[:, :], gt_hi, gt_lo, t, ht_h, -1, ht_l)
            if A:
                w.need(phi, 0, 1)
                w.need(sc_pe, -1)
                for h in range(HT):
                    last = e.tensor_scalar(q_heads[:, 0, h, :], phi_q[:, 0, :], head_col[:, h:h + 1], None, ALU.mult)
                qh0.done(last)
                cumulate(0)
                cumulate(1)
            ffn_lo(0)
            ffn_lo(1)
            if A:
                snapshot(0)
                mask(0)
            ffn_lo(2)
            if A:
                mask(1)
                reciprocals(0, 0)
            if N:
                ve_norm_x(e, w, 1)
            ffn_lo(3)
            for u in range(2, U):
                if A:
                    mask(u)
                    if u % T == 1 and u // T < C - 1:
                        snapshot(u // T)
                    reciprocals(*divmod(u - 1, C))
                if u < 6:
                    ffn_lo(u + 2)
                if N and u == 3:
                    ve_x_hat(e, w, 1)
            if A:
                reciprocals(T - 1, C - 1)
                w.need(av_pe)
                w.need(rden)
                for t in range(T):
                    attn.done(e.tensor_tensor(qk[:, t, :], num[t][:, :], qk[:, t, :], ALU.mult))
                for t in range(T):
                    ve_lo(e, w, qk[:, t, :], gt_hi, gt_lo, t, at_h, 0, at_l)
            if Fn:
                final(0)
            if A:
                w.need(e_xb)
                w.need(e_res, -1)
                for n in range(2):
                    w.need(wo_pe, 0, n)
                    cs = slice(2 * n, 2 * n + 2)
                    e_x1.done(e.tensor_tensor(x1[:, cs, :], ring_bank(f"wo{n}")[:, :].rearrange("p (c d) -> p c d", c=2),
                                              xb[:, cs, :], ALU.add))
                w.need(e_x1)
                for c in range(C):
                    last = e.bn_stats(stats2[:, c, :], x1[:, c, :])
                ln2_v.done(last)
                w.alone(ln2_v, 0, 0)
                for c in range(C):
                    last = e.bn_aggr(mv2[:, c, :], stats2[:, c, :])
                ln2_v.done(last)
                w.need(ln2_v, 0, 1)
                ln2_v.done(e.tensor_scalar(tiny[:, 0, :], mv2[:, :, 1], EPS, None, ALU.add))
                w.need(ln2_p, 0, 0)
                ln2_v.done(e.tensor_tensor(tiny[:, 2, :], tiny[:, 1, :], tiny[:, 1, :], ALU.mult))
                w.need(ln2_v, 0, 3)
                ln2_v.done(e.tensor_tensor(tiny[:, 2, :], tiny[:, 2, :], mv2[:, :, 1], ALU.mult))
                w.need(ln2_v, 0, 4)
                ln2_v.done(e.tensor_scalar(tiny[:, 3, :], tiny[:, 2, :], EPS, None, ALU.add))
                w.need(e_res, -1)
                for c in range(C):
                    last = e.tensor_scalar(hn[:, c, :], x1[:, c, :], mv2[:, c, 0:1], tiny[:, 1, c:c + 1],
                                           ALU.subtract, ALU.mult)
                e_hn.done(last)
                w.need(e_hn)
                w.need(ln2_p, 0, 1)
                w.need(ht_pe, -1)
                for c in range(C):
                    last = e.tensor_scalar(hn2[:, c, :], hn[:, c, :], tiny[:, 4, c:c + 1], None, ALU.mult)
                e_hn2.done(last)
            if N:
                for t in range(T):
                    ve_lo(e, w, ring_bank(f"xt{t}")[:, :], xt_hi, xt_lo, t, xt_h, 1, xt_l)
            if Fn:
                final(1)

        def ac_iteration(e, i, A, Fn, N):
            w = Waiter(e, i)

            def transposed_hi(use, t, pe_event, hi, shift, event):
                w.need(pe_event, shift, t)
                event.done(e.activation(hi[:, t, :], ring_bank(use)[:, :], ACT.Copy))

            def ffn(j):
                if not Fn:
                    return
                w.need(f_pe, -1, j)
                if j >= 2:
                    w.need(sl, -1, j - 2)
                else:
                    w.need(sl, -2)
                silu.done(e.activation(silu_f[:, j % 2, :], ring_bank(f"f{j}")[:, :], ACT.Silu, bias=bias_1[:, j:j + 1]))
                w.need(silu, -1, j)
                w.need(z_pe, -2)
                sh.done(e.activation(s_hi[:, j, :], silu_f[:, j % 2, :], ACT.Copy))

            if A:
                for n in range(4):
                    m, is_q = n // 2, n % 2
                    w.need(qk_pe, 0, n)
                    if n >= 2:
                        w.need(phi, 0, n - 2)
                    else:
                        w.need(phi, -1)
                    part = clip[:, n % 2, :]
                    qk_clip.done(e.activation(part, ring_bank("kq"[is_q] + str(m))[:, :], ACT.Relu,
                                              bias=bias_qkm[:, 1 - is_q, m:m + 1], scale=-1.0))
                    w.need(qk_clip, 0, n)
                    qk_exp.done(e.activation(part, part, ACT.Exp, scale=-1.0))
                for c in range(C):
                    w.need(v_pe, 0, c // 2)
                    if c == 0:
                        w.need(av_pe, -1)
                    h = c % 2
                    v_sb.done(e.activation(
                        v_pad[:, c, :, 0:4:3, :],
                        ring_bank(f"v{c // 2}")[:, h * D:(h + 1) * D].rearrange("p (r a x) -> p r a x", a=2, x=HD),
                        ACT.Copy))
            if Fn:
                for t in range(T):
                    w.need(wo_pe, -1)
                    transposed_hi(f"ht{t}", t, ht_pe, gt_hi, -1, ht_h)
            if A:
                w.need(phi, 0, 3)
                w.need(sc_pe, -1)
                for h in range(HT):
                    last = e.activation(q_heads[:, 1, h, :], phi_q[:, 1, :], ACT.Copy, scale=head_col[:, h:h + 1])
                qh1.done(last)
            ffn(0)
            ffn(1)
            if A:
                for n in range(2):
                    w.need(kt_pe, 0, n)
                    w.need(upd_pe, -1)
                    kt_sb.done(e.activation(k_tok[:, 2 * n:2 * n + 2, :],
                                            ring_bank(f"kt{n}")[:, :].rearrange("p (c d) -> p c d", c=2), ACT.Copy))
            ffn(2)
            if A:
                w.need(den_pe, 0, 0)
                den_sb.done(e.activation(qk[:, 0, :], ring_bank("den0")[:, :], ACT.Copy))
            ffn(3)
            if A:
                w.need(den_pe, 0, 1)
                den_sb.done(e.activation(qk[:, 1, :], ring_bank("den1")[:, :], ACT.Copy))
            for j in range(4, FT):
                ffn(j)
            if A:
                for t in range(T):
                    w.need(attn, 0, t)
                    w.need(f_pe, -1)
                    at_h.done(e.activation(gt_hi[:, t, :], qk[:, t, :], ACT.Copy))
            if N:
                for t in range(T):
                    w.need(v_pe, 0)
                    transposed_hi(f"xt{t}", t, xt_pe, xt_hi, 1, xt_h)

        def po_norm(e, w, s):
            w.need(ln1_ve, s)
            w.need(xhat, s - 1)
            ln1_r.done(e.tensor_tensor(rstd1[:, :], ve1[:, :], minus_half[:, :], ALU.pow))

        def po_xb(e, w, s):
            w.need(load, s)
            w.need(e_x1, s - 1)
            e_xb.done(e.tensor_tensor(xb[:, :, :], x_in[:, :, :], bias_o[:, None, :].to_broadcast([P, C, D]), ALU.add))

        def po_iteration(e, i, A, Fn, N):
            w = Waiter(e, i)
            if A:
                for t in range(T):
                    w.need(kcum, 0, t)
                    w.need(phi, 0, 2 * t + 1)
                    qkcum.done(e.tensor_tensor(qk[:, t, :], qk[:, t, :], phi_q[:, t, :], ALU.mult))
            if N:
                po_norm(e, w, 1)
            if A:
                w.need(ln2_v, 0, 2)
                ln2_p.done(e.tensor_tensor(tiny[:, 1, :], tiny[:, 0, :], minus_half[:, :], ALU.pow))
                w.need(ln2_v, 0, 5)
                ln2_p.done(e.tensor_tensor(tiny[:, 4, :], tiny[:, 3, :], minus_half[:, :], ALU.pow))
            if N:
                po_xb(e, w, 1)
            if A:
                w.need(e_hn)
                w.need(store, -1)
                res_a.done(e.tensor_tensor(res[:, :, :], x1[:, :, :], hn[:, :, :], ALU.add))
                w.need(res_a)
                e_res.done(e.tensor_tensor(res[:, :, :], res[:, :, :], bias_2[:, None, :].to_broadcast([P, C, D]), ALU.add))

        def sp_load(e, w, s, batch):
            w.need(xhat, s - 1)
            w.need(e_xb, s - 1)
            load.done(e.dma_start(x_in[:, :, :], x_v[batch]))

        def sp_iteration(e, i, A, Fn, N, N2):
            w = Waiter(e, i)
            if N2:
                sp_load(e, w, 2, i + 2)
            if Fn:
                w.need(e_out, -1)
                store.done(e.dma_start(out_v[i - 1], res[:, :, :]))

        def run(e, iteration, **kinds):
            iteration(e, 0, True, False, True)
            with e.Fori(1, B - 1) as i:
                iteration(e, i, True, True, True)
            iteration(e, B - 1, True, True, False)
            iteration(e, B, False, True, False)

        def early(e, *events):
            for v in events:
                e.sem_inc(v.sem, v.per * v.step)

        block = ctx.enter_context(nc.Block())

        WORDER = "kqvo"

        def stage_of(n):
            return stage_qkvo[n][:, 0:T, 0:D]


        @block.sync
        def _(e):
            e.dma_start(x_in[:, :, :], x_v[0]).then_inc(load.sem, 16)
            src = {"q": wq_t, "k": wk_t, "v": wv_t, "o": wo_t}
            for n in WORDER:
                e.dma_start(stage_qkvo[n][:, 0:T, 0:D] if n in "qk" else stage_qkvo[n][:, 0:T, :],
                            src[n].rearrange("(t p) n -> p t n", p=P)).then_inc(p_wdma[0], 16)
            e.dma_start(q1_i, q1.rearrange("(t p) n -> p t n", p=P)).then_inc(p_wdma[1], 16)
            for g in range(G1):
                e.dma_start(sc1_b[:, g, :], sc1[g:g + 1, :].to_broadcast([P, F])).then_inc(p_wdma[1], 16)
            e.dma_start(q2_i, q2.rearrange("(t p) n -> p t n", p=P)).then_inc(p_wdma[2], 16)
            for g in range(G2):
                e.dma_start(sc2_b[:, g, :], sc2[g:g + 1, :].to_broadcast([P, D])).then_inc(p_wdma[2], 16)
            early(e, store)
            w = Waiter(e, -1)
            sp_load(e, w, 2, 1)
            sp_iteration(e, 0, True, False, True, True)
            with e.Fori(1, B - 2) as i:
                sp_iteration(e, i, True, True, True, True)
            sp_iteration(e, B - 2, True, True, True, False)
            sp_iteration(e, B - 1, True, True, False, False)
            sp_iteration(e, B, False, True, False, False)
            e.wait_ge(store.sem, store.value(B - 1, 0))

        @block.scalar
        def _(e):
            with nc.allow_non_contiguous_dma("small bias vectors, a feature per partition"):
                for dst, src in ((bias_qk[:, 0, :], bq), (bias_qk[:, 1, :], bk), (gamma_c[:, :], gamma),
                                 (beta_c[:, :], beta), (bv_c[:, :], bv), (bias_1in[:, :], b1)):
                    e.dma_start(dst, src.rearrange("(t p) -> p t", p=P)).then_inc(p_dma, 16)
            e.dma_start(bias_o[:, :], bo.rearrange("(a d) -> a d", a=1).to_broadcast([P, D])).then_inc(p_dma, 16)
            e.dma_start(bias_2[:, :], b2.rearrange("(a d) -> a d", a=1).to_broadcast([P, D])).then_inc(p_dma, 16)
            e.wait_ge(p_wdma[0], 16 * len(WORDER))
            for n in WORDER:
                e.activation(w_hi[n][:, :, :], stage_of(n), ACT.Copy).then_inc(p_split_a, 1)
            for t in range(T):
                transposed = ring_bank(f"xt{t}")
                e.wait_ge(xt_pe.sem, t + 1)
                xt_h.done(e.activation(xt_hi[:, t, :], transposed[:, :], ACT.Copy))
            e.wait_ge(p_v, 5)
            e.activation(w1_hi[:, :, :], w1_f, ACT.Copy).then_inc(p_split_a, 1)
            e.wait_ge(p_v, 7)
            e.activation(w2_hi[:, :, :], w2_f, ACT.Copy).then_inc(p_split_a, 1)
            early(e, ht_h, silu, sh)
            run(e, ac_iteration)

        @block.gpsimd
        def _(e):
            for tile_, value in ((ident, 0.0), (head_ones, 1.0), (causal, 1.0), (head_col, 1.0)):
                e.memset(tile_[:], value).then_inc(p_const, 1)
            e.memset(ones[:, :], 1.0).then_inc(p_const, 1)
            e.memset(minus_half[:, :], -0.5).then_inc(p_const, 1)
            e.wait_ge(p_const, 6)
            n = 6

            def select(ap, compare, base, pattern, mult, fill):
                nonlocal n
                e.affine_select(out=ap, in_=ap, compare_op=compare, fill=fill, base=base, pattern=pattern,
                                channel_multiplier=mult).then_inc(p_const, 1)
                n += 1
                e.wait_ge(p_const, n)

            select(ident[:, :], ALU.not_equal, 0, [[-1, P]], 1, 1.0)
            blocks = head_ones[:, :].rearrange("p (h x) -> p h x", x=HD)
            select(blocks, ALU.is_ge, 0, [[-HD, HT], [0, HD]], 1, 0.0)
            select(blocks, ALU.is_ge, HD - 1, [[HD, HT], [0, HD]], -1, 0.0)
            select(head_col[:, :], ALU.is_ge, 0, [[-HD, HT]], 1, 0.0)
            select(head_col[:, :], ALU.is_ge, HD - 1, [[HD, HT]], -1, 0.0)
            select(causal[:, 0, :], ALU.is_ge, 0, [[1, HALF]], -1, 0.0)
            select(causal[:, 1, :], ALU.is_ge, HALF, [[1, HALF]], -1, 0.0)
            for t in range(T):
                e.tensor_copy(state_mask[:, t, :], head_ones[:, :]).then_inc(p_const, 1)
            e.memset(probs[0][:, :, :], 0.0).then_inc(p_const, 1)
            e.memset(probs[1][:, :, :], 0.0).then_inc(p_const, 1)
            e.memset(v_pad[:, :, :, :, :], 0.0).then_inc(p_const, 1)
            w = Waiter(e, -1)
            po_norm(e, w, 1)
            e.wait_ge(p_v, 9)
            po_xb(e, w, 1)
            run(e, po_iteration)

        CONSTS = 6 + 7 + T + 3

        @block.vector
        def _(e):
            e.wait_ge(p_dma, 16 * 8)
            e.tensor_scalar(bias_qk1[:, :, :], bias_qk[:, :, :], 1.0, None, ALU.add).then_inc(p_v, 1)
            e.tensor_scalar(bias_qkm[:, :, :], bias_qk[:, :, :], -1.0, None, ALU.mult).then_inc(p_v, 1)
            e.tensor_scalar(bias_2[:, :], bias_2[:, :], 0.5, None, ALU.mult).then_inc(p_v, 1)
            w = Waiter(e, -1)
            ve_norm_x(e, w, 1)
            ve_x_hat(e, w, 1)
            for k, n in enumerate(WORDER):
                e.wait_ge(p_split_a, k + 1)
                e.tensor_tensor(w_lo[n][:, :, :], stage_of(n), w_hi[n][:, :, :].bitcast(F32), ALU.subtract)\
                    .then_inc(p_split_v, 1)
            for t in range(T):
                ve_lo(e, w, ring_bank(f"xt{t}")[:, :], xt_hi, xt_lo, t, xt_h, 1, xt_l)
            e.wait_ge(p_wdma[1], 16 * (1 + G1))
            e.tensor_copy(w1_f, q1_i).then_inc(p_v, 1)
            e.wait_ge(p_v, 4)
            e.scalar_tensor_tensor(out=sc1_b, in0=w1_f, scalar=-128.0, in1=sc1_b, op0=ALU.add, op1=ALU.mult)\
                .then_inc(p_split_v, 1)
            e.wait_ge(p_split_v, 5)
            for t in range(T):
                last = e.tensor_scalar(w1_f[:, t, :], sc1_b[:, t, :], gamma_c[:, t:t + 1], None, ALU.mult)
            last.then_inc(p_v, 1)
            e.wait_ge(p_wdma[2], 16 * (1 + G2))
            e.tensor_copy(w2_f, q2_i).then_inc(p_v, 1)
            e.wait_ge(p_v, 6)
            e.scalar_tensor_tensor(out=w2_f, in0=w2_f, scalar=-128.0, in1=sc2_b, op0=ALU.add, op1=ALU.mult)\
                .then_inc(p_v, 1)
            e.wait_ge(p_split_a, 5)
            e.tensor_tensor(w1_lo[:, :, :], w1_f, w1_hi[:, :, :].bitcast(F32), ALU.subtract).then_inc(p_split_v, 1)
            e.wait_ge(p_split_a, 6)
            e.tensor_tensor(w2_lo[:, :, :], w2_f, w2_hi[:, :, :].bitcast(F32), ALU.subtract).then_inc(p_split_v, 1)
            e.wait_ge(p_pe, 1)
            e.tensor_tensor(bias_1[:, :], sc_a[:, 0:FT], bias_1in[:, :], ALU.add).then_inc(p_v, 1)
            e.wait_ge(p_pe, 2)
            e.tensor_tensor(bias_o[:, :], sc_b[:, 0:D], bias_o[:, :], ALU.add).then_inc(p_v, 1)
            e.wait_ge(p_const, CONSTS)
            e.wait_ge(p_v, 9)
            early(e, ht_l, sl, e_out)
            run(e, ve_iteration)

        @block.tensor
        def _(e):
            e.wait_ge(p_const, 7)
            w = Waiter(e, -1)
            w.need(xhat, 1)
            for t in range(T):
                for c in range(C):
                    last = e.transpose(ring_bank(f"xt{t}")[:, c * P:(c + 1) * P], x_hat[:, c, t * P:(t + 1) * P],
                                       ident[:, :])
                xt_pe.done(last)
            e.wait_ge(p_split_v, 5)
            e.wait_ge(p_dma, 16 * 8)
            for j in range(FT):
                for t in range(T):
                    last = e.matmul(sc_a[:, j:j + 1], sc1_b[:, t, j * P:(j + 1) * P], beta_c[:, t:t + 1],
                                    start=(t == 0), stop=(t == T - 1))
            last.then_inc(p_pe, 1)
            for t in range(T):
                last = e.matmul(sc_b[:, 0:D], bv_c[:, t:t + 1].to_broadcast([P, P]), stage_of("o")[:, t, :],
                                start=(t == 0), stop=(t == T - 1))
            last.then_inc(p_pe, 1)
            e.wait_ge(p_split_v, 7)
            e.wait_ge(p_v, 9)
            e.wait_ge(p_const, CONSTS)
            early(e, ht_pe, f_pe, z_pe)
            run(e, pe_iteration)


_INS = ["x", "wq_t", "bq", "wk_t", "bk", "wv_t", "bv", "wo_t", "bo", "gamma", "beta", "q1", "sc1", "b1", "q2", "sc2", "b2"]


def kernel(L0_attn_x, L0_attn_Wq, L0_attn_bq, L0_attn_Wk, L0_attn_bk, L0_attn_Wv, L0_attn_bv, L0_attn_Wo, L0_attn_bo,
           L0_ffn_ln_gamma, L0_ffn_ln_beta, L0_ffn_fc1_q, L0_ffn_fc1_scales, L0_ffn_fc1_bias,
           L0_ffn_fc2_q, L0_ffn_fc2_scales, L0_ffn_fc2_bias):
    import concourse.bacc as bacc
    from concourse.bass_utils import run_bass_kernel_spmd

    values = dict(zip(_INS, (
        L0_attn_x, np.asarray(L0_attn_Wq).T, L0_attn_bq, np.asarray(L0_attn_Wk).T, L0_attn_bk,
        np.asarray(L0_attn_Wv).T, L0_attn_bv, np.asarray(L0_attn_Wo).T, L0_attn_bo,
        L0_ffn_ln_gamma, L0_ffn_ln_beta, L0_ffn_fc1_q, L0_ffn_fc1_scales, L0_ffn_fc1_bias,
        L0_ffn_fc2_q, L0_ffn_fc2_scales, L0_ffn_fc2_bias)))
    nc = bacc.Bacc("TRN2", target_bir_lowering=False, num_devices=1)
    arrays, args = {}, []
    for name in _INS:
        a = np.ascontiguousarray(values[name])
        arrays[f"in_{name}"] = a
        args.append(nc.dram_tensor(f"in_{name}", a.shape, mybir.dt.from_np(a.dtype), kind="ExternalInput").ap())
    out = nc.dram_tensor("out", arrays["in_x"].shape, F32, kind="ExternalOutput").ap()
    build(nc, *args, out)
    r = run_bass_kernel_spmd(nc, [arrays], core_ids=[0])
    return r.results[0]["out"]
```

```python
from contextlib import ExitStack

import concourse.bass as bass
from concourse import mybir
import numpy as np

F32 = mybir.dt.float32
F32R = mybir.dt.float32r
I32 = mybir.dt.int32
ALU = mybir.AluOpType
ACT = mybir.ActivationFunctionType

P = 128
EPS = 1e-5


class Event:

    def __init__(self, sem, per, step=1, early=0):
        self.sem, self.per, self.step, self.early = sem, per, step, early

    def done(self, instruction):
        return instruction.then_inc(self.sem, self.step)

    def value(self, batch, k):
        return (batch + self.early) * (self.per * self.step) + (k + 1) * self.step


class Waiter:

    def __init__(self, engine, i):
        self.engine, self.i, self.known = engine, i, {}

    def alone(self, event, shift=0, k=None):
        self.need(event, shift, k)
        self.engine.sem_inc(self.idle, 1)

    def need(self, event, shift=0, k=None):
        k = event.per - 1 if k is None else k
        if self.known.get((id(event), shift), -1) >= k:
            return
        self.known[(id(event), shift)] = k
        value = event.value(self.i + shift, k)
        if not isinstance(value, int) or value > 0:
            self.engine.wait_ge(event.sem, value)


def build(nc, x, wq_t, bq, wk_t, bk, wv_t, bv, wo_t, bo, gamma, beta, q1, sc1, b1, q2, sc2, b2, out):
    B, S, D = x.shape
    F = q1.shape[1]
    HEADS = 16
    HD = D // HEADS
    C = S // P
    T = D // P
    HT = HEADS // T
    FT = F // P
    HALF = P // 2
    U = C * T
    HV = HT // 2
    G1, G2 = sc1.shape[0], sc2.shape[0]
    assert D == 2 * P and S == 4 * P and HD == 16 and G1 == T and G2 == FT

    x_v = x.rearrange("b (c p) d -> b p c d", p=P)
    out_v = out.rearrange("b (c p) d -> b p c d", p=P)

    with ExitStack() as ctx:
        def sb(name, shape, dtype=F32):
            return ctx.enter_context(nc.sbuf_tensor(name, shape, dtype))

        def bank(name):
            return ctx.enter_context(nc.psum_tensor(name, [P, 512], F32))

        def sem(name):
            return ctx.enter_context(nc.semaphore(name))

        w_hi = {n: sb(f"w{n}_hi", [P, T, D], F32R) for n in "qkvo"}
        w_lo = {n: sb(f"w{n}_lo", [P, T, D], F32R) for n in "qkvo"}
        w1_hi, w1_lo = sb("w1_hi", [P, T, F], F32R), sb("w1_lo", [P, T, F], F32R)
        w2_hi, w2_lo = sb("w2_hi", [P, FT, D], F32R), sb("w2_lo", [P, FT, D], F32R)
        ident = sb("ident", [P, P])
        head_ones = sb("head_ones", [P, P])
        causal = sb("causal", [P, P])
        head_col = sb("head_col", [P, HV])
        head_one = sb("head_one", [P, HT])
        ones = sb("ones", [P, 1])
        table_warm = sb("table_warm", [P, 1])
        minus_half = sb("minus_half", [P, C])
        bias_qk = sb("bias_qk", [P, 2, T])
        bias_qkm = sb("bias_qkm", [P, 2, T])
        bias_qk1 = sb("bias_qk1", [P, 2, T])
        bias_1 = sb("bias_1", [P, FT])
        bias_1in = sb("bias_1in", [P, FT])
        gamma_c, beta_c, bv_c = sb("gamma_c", [P, T]), sb("beta_c", [P, T]), sb("bv_c", [P, T])
        bias_o = sb("bias_o", [P, D])
        bias_2 = sb("bias_2", [P, D])

        x_in = sb("x_in", [P, C, D])
        xb = sb("xb", [P, C, D])
        x_hat = sb("x_hat", [P, C, D])
        xt_hi, xt_lo = sb("xt_hi", [P, T, S], F32R), sb("xt_lo", [P, T, S], F32R)
        clip = sb("clip", [P, 2, S])
        phi_q, phi_k = sb("phi_q", [P, T, S]), sb("phi_k", [P, T, S])
        qk = sb("qk", [P, T, S])
        qh_hi, qh_lo = sb("qh_hi", [P, T, HV, S], F32R), sb("qh_lo", [P, T, HV, S], F32R)
        k_hi, k_lo = sb("k_hi", [P, T, S], F32R), sb("k_lo", [P, T, S], F32R)
        k_tok = sb("k_tok", [P, C, D])
        v_pad = sb("v_pad", [P, C, HT * T // 2, 4, HD])
        probs = [sb(f"probs{n}", [P, HT, P]) for n in range(2)]
        state = sb("state", [P, 2, T, P])
        gt_hi, gt_lo = sb("gt_hi", [P, T, S], F32R), sb("gt_lo", [P, T, S], F32R)
        x1 = sb("x1", [P, C, D])
        hn2 = sb("hn2", [P, C, D])
        res = sb("res", [P, C, D])
        silu_f = sb("silu_f", [P, 2, S])
        s_hi, s_lo = sb("s_hi", [P, FT, S], F32R), sb("s_lo", [P, FT, S], F32R)
        stats1, stats2 = sb("stats1", [P, C, 6]), sb("stats2", [P, C, 6])
        mv1, mv2 = sb("mv1", [P, C, 2]), sb("mv2", [P, C, 2])
        ve1, rstd1 = sb("ve1", [P, C]), sb("rstd1", [P, C])
        tiny = sb("tiny", [P, 6, C])
        stage_qkvo = {n: t for n, t in zip("qkvo", (phi_q, phi_k, k_tok, x1))}
        def flat(tile_):
            return tile_[:].rearrange("p a n -> p (a n)")

        def groups(ap, n):
            return ap.rearrange("p (g n) -> p g n", n=n)

        v_flat = v_pad[:, :, :, :, :].rearrange("p c r a x -> p (c r a x)")
        w1_f = [v_flat[:, t * F:(t + 1) * F] for t in range(T)]
        w1_raw = [flat(probs[0]), flat(hn2)]
        w2_f = [groups(flat(qk), D), groups(flat(res), D)]
        sc2_b = [groups(flat(clip), D), groups(flat(silu_f), D)]

        num = [bank(f"num{t}") for t in range(T)]
        state_acc = bank("state_acc")
        sc = [bank(f"sc{r}") for r in range(2)]
        ring = [bank(f"ring{n}") for n in range(3)]
        USES = ["ht0", "v1", "ht1", "f0", "f1", "f2", "den0", "f3", "den1", "f4", "f5", "f6", "f7",
                "xt0", "xt1", "z0", "z1", "wo0", "wo1"]
        BORROWED = {"v0": state_acc, "kt0": sc[0], "kt1": sc[1]}
        FFN_USES = {"ht0", "ht1", "z0", "z1"} | {f"f{j}" for j in range(FT)}

        def qk_bank(is_q, m):
            return (sc, num)[m][is_q]

        def ring_bank(use):
            return BORROWED[use] if use in BORROWED else ring[USES.index(use) % 3]

        def ev(name, per, **more):
            return Event(sem(name), per, **more)

        load = ev("load", 1, step=16)
        ln1_st = ev("ln1_st", 1)
        ln1_mv = ev("ln1_mv", 1)
        ln1_ve = ev("ln1_ve", 1)
        ln1_r = ev("ln1_r", 1)
        xhat = ev("xhat", 1)
        e_xb = ev("e_xb", 1)
        xt_pe, xt_h, xt_l = ev("xt_pe", T), ev("xt_h", T), ev("xt_l", T)
        qk_pe, qk_exp, qk_clip, phi = ev("qk_pe", 2 * T), ev("qk_exp", 2 * T), ev("qk_clip", 2 * T), ev("phi", 2 * T)
        v_pe, v_sb = ev("v_pe", C // 2), ev("v_sb", C)
        kt_pe, kt_sb = ev("kt_pe", C // 2), ev("kt_sb", C // 2)
        kcum, qkcum = ev("kcum", T), ev("qkcum", T)
        e_kh, e_kl, e_qh, e_ql = ev("e_kh", T), ev("e_kl", T), ev("e_qh", T), ev("e_ql", T)
        sc_pe, masked = ev("sc_pe", U), ev("masked", 2 * U)
        upd_pe, snap = ev("upd_pe", C - 1), ev("snap", C - 1)
        av_pe = ev("av_pe", U)
        den_pe, den_sb, rden = ev("den_pe", T), ev("den_sb", T), ev("rden", U)
        attn, at_h, at_l = ev("attn", T), ev("at_h", T), ev("at_l", T)
        wo_pe, e_x1 = ev("wo_pe", C // 2), ev("e_x1", C // 2)
        ln2_v = ev("ln2_v", 7)
        ln2_p = ev("ln2_p", 2)
        e_hn2 = ev("e_hn2", 1)
        F_ = dict(early=1)
        e_hn, res_a, e_res = ev("e_hn", 1, **F_), ev("res_a", 1, **F_), ev("e_res", 1, **F_)
        ht_pe, ht_h, ht_l = ev("ht_pe", T, **F_), ev("ht_h", T, **F_), ev("ht_l", T, **F_)
        f_pe, silu, sh, sl = ev("f_pe", FT, **F_), ev("silu", FT, **F_), ev("sh", FT, **F_), ev("sl", FT, **F_)
        z_pe, e_out = ev("z_pe", C // 2, **F_), ev("e_out", C // 2, **F_)
        store = ev("store", 2, step=16, **F_)

        Waiter.idle = sem("idle")
        p_const, p_dma, p_wdma = sem("p_const"), sem("p_dma"), [sem(f"p_wdma{n}") for n in range(3)]
        p_split_a, p_split_v, p_v, p_pe, p_a = sem("p_split_a"), sem("p_split_v"), sem("p_v"), sem("p_pe"), sem("p_a")

        LAST_READ = {
            "v1": (v_sb, 3), "ht0": (ht_l, 0), "ht1": (ht_l, 1), "den0": (den_sb, 0),
            "den1": (den_sb, 1), "z0": (e_out, 0), "z1": (e_out, 1), "wo0": (e_x1, 0), "wo1": (e_x1, 1),
            "xt0": (xt_l, 0), "xt1": (xt_l, 1),
        } | {f"f{j}": (silu, j) for j in range(FT)}

        def batch_shift(use):
            return -1 if use in FFN_USES else 1 if use in ("xt0", "xt1") else 0

        def free_bank(w, use, present):
            if use == "v0":
                w.need(snap, -1)
                return
            if use in BORROWED:
                w.need(phi, 0, int(use[-1]))
                return
            n = USES.index(use)
            m = n - 1
            while True:
                earlier = m < 0
                other = USES[m % len(USES)]
                shift = batch_shift(other) - earlier
                exists = other in present or (earlier and not (isinstance(w.i, int) and w.i + shift >= B))
                if USES.index(other) % 3 == USES.index(use) % 3 and exists:
                    event, k = LAST_READ[other]
                    w.need(event, shift, k)
                    return
                m -= 1

        def pe_split3(e, target, pairs):
            n = 0
            for (lh, ll), (rh, rl) in pairs:
                for a, b in ((lh, rh), (lh, rl), (ll, rh)):
                    last = e.matmul(target, a, b, start=(n == 0), stop=(n == 3 * len(pairs) - 1))
                    n += 1
            return last

        def pe_projection(e, w, n, m, s):
            if m:
                w.need(attn, s - 1)
            else:
                w.need(masked, s - 1)
            cols = slice(m * P, (m + 1) * P)
            last = pe_split3(e, qk_bank("kq".index(n), m)[:, :], [
                ((w_hi[n][:, t, cols], w_lo[n][:, t, cols]), (xt_hi[:, t, :], xt_lo[:, t, :])) for t in range(T)])
            qk_pe.done(last)

        def pe_tokens(e, w, n, lhs, use, present, event):
            free_bank(w, use, present)
            for h in range(2):
                toks = slice((2 * int(use[-1]) + h) * P, (2 * int(use[-1]) + h + 1) * P)
                last = pe_split3(e, ring_bank(use)[:, h * D:(h + 1) * D], [
                    ((lhs[0][:, t, toks], lhs[1][:, t, toks]), (w_hi[n][:, t, :], w_lo[n][:, t, :])) for t in range(T)])
            event.done(last)

        def pe_transposes(e, w, src, t, use, present, event):
            free_bank(w, use, present)
            for c in range(C):
                last = e.transpose(ring_bank(use)[:, c * P:(c + 1) * P], src[:, c, t * P:(t + 1) * P], ident[:, :])
            event.done(last)

        def pe_iteration(e, i, A, Fn, N):
            w = Waiter(e, i)
            present = {u for u in USES if (Fn if u in FFN_USES else N if u in ("xt0", "xt1") else A)}

            def x_transposes():
                w.need(xhat, 1)
                for t in range(T):
                    pe_transposes(e, w, x_hat, t, f"xt{t}", present, xt_pe)

            def ffn_in():
                w.need(e_hn2, -1)
                for t in range(T):
                    pe_transposes(e, w, hn2, t, f"ht{t}", present, ht_pe)

            def fc1(j):
                if not Fn:
                    return
                w.need(ht_l, -1)
                free_bank(w, f"f{j}", present)
                cols = slice(j * P, (j + 1) * P)
                f_pe.done(pe_split3(e, ring_bank(f"f{j}")[:, :], [
                    ((w1_hi[:, t, cols], w1_lo[:, t, cols]), (gt_hi[:, t, :], gt_lo[:, t, :])) for t in range(T)]))

            def fc2(c):
                if not Fn:
                    return
                w.need(sh, -1)
                w.need(sl, -1)
                n, h = divmod(c, 2)
                if h == 0:
                    free_bank(w, f"z{n}", present)
                toks = slice(c * P, (c + 1) * P)
                last = pe_split3(e, ring_bank(f"z{n}")[:, h * D:(h + 1) * D], [
                    ((s_hi[:, j, toks], s_lo[:, j, toks]), (w2_hi[:, j, :], w2_lo[:, j, :])) for j in range(FT)])
                if h:
                    z_pe.done(last)

            def k_transposes(n):
                w.need(phi, 0, 2)
                free_bank(w, f"kt{n}", present)
                for h in range(2):
                    for t in range(T):
                        c = 2 * n + h
                        last = e.transpose(ring_bank(f"kt{n}")[:, (h * T + t) * P:(h * T + t + 1) * P],
                                           phi_k[:, t, c * P:(c + 1) * P], ident[:, :])
                kt_pe.done(last)

            def scores(u):
                c, t = divmod(u, T)
                w.need(e_kl, 0, t)
                w.need(e_ql, 0, t)
                w.need(*((masked, 0, 2 * u - 1) if u else (kt_sb, 0)))
                toks = slice(c * P, (c + 1) * P)
                for n, (ks, qs) in enumerate(((k_hi, qh_hi), (k_hi, qh_lo), (k_lo, qh_hi))):
                    for r in range(2):
                        half = slice(r * HALF, (r + 1) * HALF)
                        last = e.matmul(sc[r][:, :], ks[half, t, toks], qs[half, t, :, toks],
                                        start=(n == 0), stop=(n == 2))
                sc_pe.done(last)

            def from_state(u):
                c, t = divmod(u, T)
                if c:
                    w.need(snap, 0, c - 1)
                    e.matmul(num[t][:, c * P:(c + 1) * P], state[:, (c - 1) % 2, t, :], phi_q[:, t, c * P:(c + 1) * P],
                             start=False, stop=False, skip_group_check=True)

            def update_state(c):
                w.need(kt_sb, 0, c // 2)
                w.need(v_sb, 0, max(c, 1))
                if c:
                    w.need(snap, 0, c - 1)
                for t in range(T):
                    last = e.matmul(state_acc[:, t * P:(t + 1) * P], k_tok[:, c, t * P:(t + 1) * P],
                                    v_pad[:, c, t * HT // 2:(t + 1) * HT // 2, 0:4:3, :],
                                    start=(c == 0 and t == 0), stop=True, skip_group_check=True)
                upd_pe.done(last)

            def values(u):
                c, t = divmod(u, T)
                w.need(masked, 0, 2 * u + 1)
                w.need(v_sb, 0, c)
                if c == 0:
                    w.need(attn, -1)
                for odd in range(2):
                    for pair in range(HT // 2):
                        last = e.matmul(
                            num[t][32 * pair:32 * pair + 32, c * P:(c + 1) * P],
                            v_pad[:, c, t * HT // 2 + pair, 2 * odd:2 * odd + 2, :],
                            probs[u % 2][:, 2 * pair + odd, :],
                            start=(c == 0 and odd == 0), stop=(odd == 1), skip_group_check=True)
                av_pe.done(last)

            def denominator(t):
                w.need(qkcum, 0, t)
                free_bank(w, f"den{t}", present)
                den_pe.done(e.matmul(ring_bank(f"den{t}")[:, :], head_ones[:, :], qk[:, t, :], start=True, stop=True))

            def project_v(n):
                if A:
                    w.need(xt_l)
                    pe_tokens(e, w, "v", (xt_hi, xt_lo), f"v{n}", present, v_pe)

            project_v(0)
            if Fn:
                ffn_in()
            project_v(1)
            if A:
                k_transposes(0)
                k_transposes(1)
            fc1(0)
            fc1(1)
            fc1(2)
            if A:
                update_state(0)
                scores(0)
                denominator(0)
            fc1(3)
            if A:
                scores(1)
                values(0)
                denominator(1)
            for u in range(2, U):
                if u < 6:
                    fc1(u + 2)
                elif u == 6 and N:
                    x_transposes()
                elif u == 7:
                    fc2(0)
                if A:
                    if u % T == 0 and u // T < C - 1:
                        update_state(u // T)
                    scores(u)
                    from_state(u - 1)
                    values(u - 1)
            fc2(1)
            if A:
                from_state(U - 1)
                values(U - 1)
            fc2(2)
            if A:
                w.need(at_l)
                for n in range(2):
                    pe_tokens(e, w, "o", (gt_hi, gt_lo), f"wo{n}", present, wo_pe)
            if N:
                w.need(xt_l, 1)
                for m in range(T):
                    pe_projection(e, w, "k", m, 1)
                    pe_projection(e, w, "q", m, 1)
            fc2(3)

        def ve_norm_x(e, w, s):
            w.need(load, s)
            for c in range(C):
                last = e.bn_stats(stats1[:, c, :], x_in[:, c, :])
            ln1_st.done(last)
            w.alone(ln1_st, s)
            for c in range(C):
                last = e.bn_aggr(mv1[:, c, :], stats1[:, c, :])
            ln1_mv.done(last)
            w.need(ln1_mv, s)
            ln1_ve.done(e.tensor_scalar(ve1[:, :], mv1[:, :, 1], EPS, None, ALU.add))

        def ve_x_hat(e, w, s):
            w.need(ln1_r, s)
            w.need(xt_pe, s - 1)
            for c in range(C):
                last = e.tensor_scalar(x_hat[:, c, :], x_in[:, c, :], mv1[:, c, 0:1], rstd1[:, c:c + 1],
                                       ALU.subtract, ALU.mult)
            xhat.done(last)

        def ve_lo(e, w, bank_, hi, lo, t, hi_event, shift, event):
            w.need(hi_event, shift, t)
            event.done(e.tensor_tensor(lo[:, t, :], bank_, hi[:, t, :].bitcast(F32), ALU.subtract))

        def ve_iteration(e, i, A, Fn, N):
            w = Waiter(e, i)

            def features(n, s):
                m, is_q = n // 2, n % 2
                w.need(qk_exp, s, n)
                w.need(av_pe, s - 1)
                dst = phi_q if is_q else phi_k
                phi.done(e.scalar_tensor_tensor(
                    out=dst[:, m, :], in0=qk_bank(is_q, m)[:, :], scalar=bias_qk1[:, 1 - is_q, m:m + 1],
                    in1=clip[:, n % 2, :], op0=ALU.add, op1=ALU.max))

            def features_(n):
                if N:
                    features(n, 1)

            def cumulate(t, s):
                w.need(phi, s, 2 * t)
                w.need(attn, s - 1)
                kcum.done(e.tensor_tensor_scan(qk[:, t, :], ones[:, 0:1].to_broadcast([P, S]), phi_k[:, t, :], 0.0,
                                               ALU.mult, ALU.add))

            def split_lo(t):
                w.need(sc_pe, -1)
                w.need(e_kh, 0, t)
                e_kl.done(e.tensor_tensor(k_lo[:, t, :], phi_k[:, t, :], k_hi[:, t, :].bitcast(F32), ALU.subtract))
                w.need(e_qh, 0, t)
                for v in range(HV):
                    last = e.scalar_tensor_tensor(
                        out=qh_lo[:, t, v, :], in0=phi_q[:, t, :], scalar=head_col[:, v:v + 1],
                        in1=qh_hi[:, t, v, :].bitcast(F32), op0=ALU.mult, op1=ALU.subtract)
                e_ql.done(last)

            def ffn_lo(j):
                if not Fn:
                    return
                w.need(sh, -1, j)
                w.need(z_pe, -2)
                sl.done(e.tensor_tensor(s_lo[:, j, :], silu_f[:, j % 2, :], s_hi[:, j, :].bitcast(F32), ALU.subtract))

            def mask(u):
                w.need(sc_pe, 0, u)
                if u >= 2:
                    w.need(av_pe, 0, u - 2)
                else:
                    w.need(av_pe, -1)
                for r in range(2):
                    masked.done(e.tensor_tensor(
                        probs[u % 2][:, r * HV:(r + 1) * HV, :], sc[r][:, :].rearrange("p (h q) -> p h q", h=HV),
                        causal[:, None, :].to_broadcast([P, HV, P]), ALU.mult))

            def snapshot(c):
                w.need(upd_pe, 0, c)
                if c >= 2:
                    w.need(av_pe, 0, T * c - 1)
                else:
                    w.need(av_pe, -1)
                snap.done(e.tensor_tensor(state[:, c % 2, :, :], state_acc[:, 0:T * P].rearrange("p (t f) -> p t f", t=T),
                                          head_ones[:, None, :].to_broadcast([P, T, P]), ALU.mult))

            def reciprocals(t, n):
                w.need(den_sb, 0, t)
                part = qk[:, t, n * P:(n + 1) * P]
                rden.done(e.reciprocal(part, part))

            def final(n):
                w.need(z_pe, -1, n)
                w.need(e_res, -1)
                cs = slice(2 * n, 2 * n + 2)
                e_out.done(e.scalar_tensor_tensor(
                    out=res[:, cs, :], in0=ring_bank(f"z{n}")[:, :].rearrange("p (c d) -> p c d", c=2), scalar=0.5,
                    in1=res[:, cs, :], op0=ALU.mult, op1=ALU.add))

            if Fn:
                for t in range(T):
                    ve_lo(e, w, ring_bank(f"ht{t}")[:, :], gt_hi, gt_lo, t, ht_h, -1, ht_l)
            if A:
                split_lo(0)
                split_lo(1)
            ffn_lo(0)
            if A:
                snapshot(0)
                mask(0)
            ffn_lo(1)
            if Fn:
                w.need(store, -2)
                for c in range(C):
                    last = e.tensor_scalar(res[:, c, :], x1[:, c, :], mv2[:, c, 0:1], tiny[:, 1, c:c + 1],
                                           ALU.subtract, ALU.mult)
                e_hn.done(last)
            ffn_lo(2)
            if A:
                mask(1)
                reciprocals(0, 0)
            if N:
                ve_norm_x(e, w, 1)
            ffn_lo(3)
            for u in range(2, U):
                if A:
                    if u == U - 1:
                        reciprocals(T - 1, C - 1)
                    mask(u)
                    if u % T == 1 and u // T < C - 1:
                        snapshot(u // T)
                    reciprocals(*divmod(u - 1, C))
                if u < 6:
                    ffn_lo(u + 2)
                if N and u == 3:
                    ve_x_hat(e, w, 1)
            def attention(t):
                w.need(rden)
                w.need(av_pe, 0, U - T + t)
                attn.done(e.tensor_tensor(qk[:, t, :], num[t][:, :], qk[:, t, :], ALU.mult))

            if A:
                attention(0)
            if N:
                for t in range(T):
                    ve_lo(e, w, ring_bank(f"xt{t}")[:, :], xt_hi, xt_lo, t, xt_h, 1, xt_l)
            if A:
                ve_lo(e, w, qk[:, 0, :], gt_hi, gt_lo, 0, at_h, 0, at_l)
                attention(1)
                ve_lo(e, w, qk[:, 1, :], gt_hi, gt_lo, 1, at_h, 0, at_l)
            if Fn:
                final(0)
            if A:
                w.need(e_xb)
                w.need(e_res, -1)
                for n in range(2):
                    w.need(wo_pe, 0, n)
                    cs = slice(2 * n, 2 * n + 2)
                    e_x1.done(e.tensor_tensor(x1[:, cs, :], ring_bank(f"wo{n}")[:, :].rearrange("p (c d) -> p c d", c=2),
                                              xb[:, cs, :], ALU.add))
                w.need(e_x1)
                for c in range(C):
                    last = e.bn_stats(stats2[:, c, :], x1[:, c, :])
                ln2_v.done(last)
                w.alone(ln2_v, 0, 0)
                for c in range(C):
                    last = e.bn_aggr(mv2[:, c, :], stats2[:, c, :])
                ln2_v.done(last)
                w.need(ln2_v, 0, 1)
                ln2_v.done(e.tensor_scalar(tiny[:, 0, :], mv2[:, :, 1], EPS, None, ALU.add))
                features_(0)
                w.need(ln2_p, 0, 0)
                ln2_v.done(e.tensor_tensor(tiny[:, 2, :], tiny[:, 1, :], tiny[:, 1, :], ALU.mult))
                w.need(ln2_v, 0, 3)
                ln2_v.done(e.tensor_tensor(tiny[:, 2, :], tiny[:, 2, :], mv2[:, :, 1], ALU.mult))
                w.need(ln2_v, 0, 4)
                ln2_v.done(e.tensor_scalar(tiny[:, 3, :], tiny[:, 2, :], EPS, None, ALU.add))
                features_(1)
                w.need(ln2_p, 0, 1)
                ln2_v.done(e.tensor_tensor(tiny[:, 5, :], tiny[:, 4, :], tiny[:, 1, :], ALU.mult))
                w.need(ln2_v)
                w.need(ht_pe, -1)
                for c in range(C):
                    last = e.tensor_scalar(hn2[:, c, :], x1[:, c, :], mv2[:, c, 0:1], tiny[:, 5, c:c + 1],
                                           ALU.subtract, ALU.mult)
                e_hn2.done(last)
            else:
                features_(0)
                features_(1)
            features_(2)
            features_(3)
            if Fn:
                final(1)
            if N:
                cumulate(0, 1)
                cumulate(1, 1)

        def ac_iteration(e, i, A, Fn, N):
            w = Waiter(e, i)

            def transposed_hi(use, t, pe_event, hi, shift, event):
                w.need(pe_event, shift, t)
                event.done(e.activation(hi[:, t, :], ring_bank(use)[:, :], ACT.Copy))

            def ffn(j):
                if not Fn:
                    return
                w.need(f_pe, -1, j)
                if j >= 2:
                    w.need(sl, -1, j - 2)
                else:
                    w.need(sl, -2)
                silu.done(e.activation(silu_f[:, j % 2, :], ring_bank(f"f{j}")[:, :], ACT.Silu, bias=bias_1[:, j:j + 1]))
                w.need(silu, -1, j)
                w.need(z_pe, -2)
                sh.done(e.activation(s_hi[:, j, :], silu_f[:, j % 2, :], ACT.Copy))

            def split_hi(t):
                w.need(sc_pe, -1)
                w.need(phi, 0, 2 * t + 1)
                e_kh.done(e.activation(k_hi[:, t, :], phi_k[:, t, :], ACT.Copy))
                for v in range(HV):
                    last = e.activation(qh_hi[:, t, v, :], phi_q[:, t, :], ACT.Copy, scale=head_col[:, v:v + 1])
                e_qh.done(last)

            def exponentials(s):
                for n in range(4):
                    m, is_q = n // 2, n % 2
                    w.need(qk_pe, s, n)
                    if n >= 2:
                        w.need(phi, s, n - 2)
                    else:
                        w.need(phi, s - 1)
                    part = clip[:, n % 2, :]
                    qk_clip.done(e.activation(part, qk_bank(is_q, m)[:, :], ACT.Relu,
                                              bias=bias_qkm[:, 1 - is_q, m:m + 1], scale=-1.0))
                    w.need(qk_clip, s, n)
                    qk_exp.done(e.activation(part, part, ACT.Exp, scale=-1.0))

            if A:
                split_hi(0)
            if Fn:
                for t in range(T):
                    w.need(wo_pe, -1)
                    transposed_hi(f"ht{t}", t, ht_pe, gt_hi, -1, ht_h)
            if A:
                for c in range(C):
                    w.need(v_pe, 0, c // 2)
                    if c == 0:
                        w.need(av_pe, -1)
                    h = c % 2
                    v_sb.done(e.activation(
                        v_pad[:, c, :, 0:4:3, :],
                        ring_bank(f"v{c // 2}")[:, h * D:(h + 1) * D].rearrange("p (r a x) -> p r a x", a=2, x=HD),
                        ACT.Copy))
            if A:
                for n in range(2):
                    w.need(kt_pe, 0, n)
                    w.need(upd_pe, -1)
                    kt_sb.done(e.activation(k_tok[:, 2 * n:2 * n + 2, :],
                                            ring_bank(f"kt{n}")[:, :].rearrange("p (c d) -> p c d", c=2), ACT.Copy))
            if A:
                split_hi(1)
            ffn(0)
            ffn(1)
            ffn(2)
            if A:
                w.need(den_pe, 0, 0)
                den_sb.done(e.activation(qk[:, 0, :], ring_bank("den0")[:, :], ACT.Copy))
            ffn(3)
            if A:
                w.need(den_pe, 0, 1)
                den_sb.done(e.activation(qk[:, 1, :], ring_bank("den1")[:, :], ACT.Copy))
            for j in range(4, FT):
                ffn(j)
            if N:
                for t in range(T):
                    w.need(v_pe, 0)
                    transposed_hi(f"xt{t}", t, xt_pe, xt_hi, 1, xt_h)
            if A:
                for t in range(T):
                    w.need(attn, 0, t)
                    w.need(f_pe, -1)
                    at_h.done(e.activation(gt_hi[:, t, :], qk[:, t, :], ACT.Copy))
            if N:
                e.activation(table_warm[:, 0:1], ones[:, 0:1], ACT.Exp)
                exponentials(1)

        def po_norm(e, w, s):
            w.need(ln1_ve, s)
            w.need(xhat, s - 1)
            ln1_r.done(e.tensor_tensor(rstd1[:, :], ve1[:, :], minus_half[:, :], ALU.pow))

        def po_xb(e, w, s):
            w.need(load, s)
            w.need(e_x1, s - 1)
            e_xb.done(e.tensor_tensor(xb[:, :, :], x_in[:, :, :], bias_o[:, None, :].to_broadcast([P, C, D]), ALU.add))

        def po_iteration(e, i, A, Fn, N):
            w = Waiter(e, i)
            if Fn:
                w.need(e_hn, -1)
                res_a.done(e.tensor_tensor(res[:, :, :], x1[:, :, :], res[:, :, :], ALU.add))
                w.need(res_a, -1)
                e_res.done(e.tensor_tensor(res[:, :, :], res[:, :, :], bias_2[:, None, :].to_broadcast([P, C, D]), ALU.add))
            if N:
                po_norm(e, w, 1)
            if A:
                w.need(ln2_v, 0, 2)
                ln2_p.done(e.tensor_tensor(tiny[:, 1, :], tiny[:, 0, :], minus_half[:, :], ALU.pow))
                w.need(ln2_v, 0, 5)
                ln2_p.done(e.tensor_tensor(tiny[:, 4, :], tiny[:, 3, :], minus_half[:, :], ALU.pow))
            if N:
                for t in range(T):
                    w.need(kcum, 1, t)
                    w.need(phi, 1, 2 * t + 1)
                    qkcum.done(e.tensor_tensor(qk[:, t, :], qk[:, t, :], phi_q[:, t, :], ALU.mult))
                po_xb(e, w, 1)

        def sp_load(e, w, s, batch):
            w.need(xhat, s - 1)
            w.need(e_xb, s - 1)
            load.done(e.dma_start(x_in[:, :, :], x_v[batch]))

        def sp_iteration(e, i, A, Fn, N, N2):
            w = Waiter(e, i)
            if N2:
                sp_load(e, w, 2, i + 2)
            if Fn:
                for n in range(2):
                    w.need(e_out, -1, n)
                    cs = slice(2 * n, 2 * n + 2)
                    store.done(e.dma_start(out_v[i - 1][:, cs, :], res[:, cs, :]))

        def run(e, iteration, **kinds):
            iteration(e, -1, False, False, True)
            iteration(e, 0, True, False, True)
            with e.Fori(1, B - 1) as i:
                iteration(e, i, True, True, True)
            iteration(e, B - 1, True, True, False)
            iteration(e, B, False, True, False)

        def early(e, *events):
            for v in events:
                e.sem_inc(v.sem, v.per * v.step)

        block = ctx.enter_context(nc.Block())

        WORDER = "kqvo"

        def stage_of(n):
            return stage_qkvo[n][:, 0:T, 0:D]


        @block.sync
        def _(e):
            e.dma_start(x_in[:, :, :], x_v[0]).then_inc(load.sem, 16)
            src = {"q": wq_t, "k": wk_t, "v": wv_t, "o": wo_t}
            for n in WORDER:
                e.dma_start(stage_qkvo[n][:, 0:T, 0:D] if n in "qk" else stage_qkvo[n][:, 0:T, :],
                            src[n].rearrange("(t p) n -> p t n", p=P)).then_inc(p_wdma[0], 16)
            for t in range(T):
                e.dma_start(w1_f[t].bitcast(I32), q1[t * P:(t + 1) * P, :]).then_inc(p_wdma[1], 16)
                e.dma_start(w1_raw[t], sc1[t:t + 1, :].to_broadcast([P, F])).then_inc(p_wdma[1], 16)
            for n in range(2):
                e.dma_start(w2_f[n].bitcast(I32), q2[n * F // 2:(n + 1) * F // 2, :].rearrange("(g p) n -> p g n", p=P))\
                    .then_inc(p_wdma[2], 16)
                for g in range(FT // 2):
                    e.dma_start(sc2_b[n][:, g, :], sc2[n * FT // 2 + g:n * FT // 2 + g + 1, :].to_broadcast([P, D]))\
                        .then_inc(p_wdma[2], 16)
            early(e, store)
            w = Waiter(e, -1)
            sp_load(e, w, 2, 1)
            sp_iteration(e, 0, True, False, True, True)
            with e.Fori(1, B - 2) as i:
                sp_iteration(e, i, True, True, True, True)
            sp_iteration(e, B - 2, True, True, True, False)
            sp_iteration(e, B - 1, True, True, False, False)
            sp_iteration(e, B, False, True, False, False)
            e.wait_ge(store.sem, store.value(B - 1, 1))

        @block.scalar
        def _(e):
            with nc.allow_non_contiguous_dma("small bias vectors, a feature per partition"):
                for dst, src in ((bias_qk[:, 0, :], bq), (bias_qk[:, 1, :], bk), (gamma_c[:, :], gamma),
                                 (beta_c[:, :], beta), (bv_c[:, :], bv), (bias_1in[:, :], b1)):
                    e.dma_start(dst, src.rearrange("(t p) -> p t", p=P)).then_inc(p_dma, 16)
            e.dma_start(bias_o[:, :], bo.rearrange("(a d) -> a d", a=1).to_broadcast([P, D])).then_inc(p_dma, 16)
            e.dma_start(bias_2[:, :], b2.rearrange("(a d) -> a d", a=1).to_broadcast([P, D])).then_inc(p_dma, 16)
            e.wait_ge(p_wdma[0], 16 * len(WORDER))
            for n in WORDER:
                e.activation(w_hi[n][:, :, :], stage_of(n), ACT.Copy).then_inc(p_split_a, 1)
            e.wait_ge(p_v, 5)
            for t in range(T):
                e.activation(w1_hi[:, t, :], w1_f[t], ACT.Copy).then_inc(p_split_a, 1)
            e.wait_ge(p_v, 7)
            for n in range(2):
                e.activation(w2_hi[:, n * FT // 2:(n + 1) * FT // 2, :], w2_f[n], ACT.Copy).then_inc(p_split_a, 1)
            early(e, ht_h, silu, sh)
            run(e, ac_iteration)

        @block.gpsimd
        def _(e):
            for tile_, value in ((ident, 0.0), (head_ones, 1.0), (causal, 1.0), (head_one, 1.0)):
                e.memset(tile_[:], value).then_inc(p_const, 1)
            e.memset(ones[:, :], 1.0).then_inc(p_const, 1)
            e.memset(minus_half[:, :], -0.5).then_inc(p_const, 1)
            e.wait_ge(p_const, 6)
            n = 6

            def select(ap, compare, base, pattern, mult, fill):
                nonlocal n
                e.affine_select(out=ap, in_=ap, compare_op=compare, fill=fill, base=base, pattern=pattern,
                                channel_multiplier=mult).then_inc(p_const, 1)
                n += 1
                e.wait_ge(p_const, n)

            select(ident[:, :], ALU.not_equal, 0, [[-1, P]], 1, 1.0)
            blocks = head_ones[:, :].rearrange("p (h x) -> p h x", x=HD)
            select(blocks, ALU.is_ge, 0, [[-HD, HT], [0, HD]], 1, 0.0)
            select(blocks, ALU.is_ge, HD - 1, [[HD, HT], [0, HD]], -1, 0.0)
            select(head_one[:, :], ALU.is_ge, 0, [[-HD, HT]], 1, 0.0)
            select(head_one[:, :], ALU.is_ge, HD - 1, [[HD, HT]], -1, 0.0)
            select(causal[:, :], ALU.is_ge, 0, [[1, P]], -1, 0.0)
            e.tensor_tensor(head_col[:, :], head_one[:, 0:HV], head_one[:, HV:HT], ALU.add).then_inc(p_const, 1)
            e.wait_ge(p_split_v, 7)
            e.memset(v_pad[:, :, :, :, :], 0.0).then_inc(p_const, 1)
            e.wait_ge(p_v, 9)
            early(e, res_a, e_res)
            run(e, po_iteration)

        CONSTS = 6 + 6 + 1 + 1

        @block.vector
        def _(e):
            e.wait_ge(p_dma, 16 * 8)
            e.tensor_scalar(bias_qk1[:, :, :], bias_qk[:, :, :], 1.0, None, ALU.add).then_inc(p_v, 1)
            e.tensor_scalar(bias_qkm[:, :, :], bias_qk[:, :, :], -1.0, None, ALU.mult).then_inc(p_v, 1)
            e.tensor_scalar(bias_2[:, :], bias_2[:, :], 0.5, None, ALU.mult).then_inc(p_v, 1)
            for k, n in enumerate(WORDER):
                e.wait_ge(p_split_a, k + 1)
                e.tensor_tensor(w_lo[n][:, :, :], stage_of(n), w_hi[n][:, :, :].bitcast(F32), ALU.subtract)\
                    .then_inc(p_split_v, 1)
            e.wait_ge(p_wdma[1], 16 * 2 * T)
            for t in range(T):
                last = e.tensor_copy(w1_f[t], w1_f[t].bitcast(I32))
            last.then_inc(p_v, 1)
            e.wait_ge(p_v, 4)
            for t in range(T):
                last = e.scalar_tensor_tensor(out=w1_raw[t], in0=w1_f[t], scalar=-128.0, in1=w1_raw[t],
                                              op0=ALU.add, op1=ALU.mult)
            last.then_inc(p_split_v, 1)
            e.wait_ge(p_split_v, 5)
            for t in range(T):
                last = e.tensor_scalar(w1_f[t], w1_raw[t], gamma_c[:, t:t + 1], None, ALU.mult)
            last.then_inc(p_v, 1)
            e.wait_ge(p_wdma[2], 16 * (2 + G2))
            for n in range(2):
                last = e.tensor_copy(w2_f[n], w2_f[n].bitcast(I32))
            last.then_inc(p_v, 1)
            e.wait_ge(p_v, 6)
            for n in range(2):
                last = e.scalar_tensor_tensor(out=w2_f[n], in0=w2_f[n], scalar=-128.0, in1=sc2_b[n],
                                              op0=ALU.add, op1=ALU.mult)
            last.then_inc(p_v, 1)
            for t in range(T):
                e.wait_ge(p_split_a, 5 + t)
                last = e.tensor_tensor(w1_lo[:, t, :], w1_f[t], w1_hi[:, t, :].bitcast(F32), ALU.subtract)
            last.then_inc(p_split_v, 1)
            for n in range(2):
                e.wait_ge(p_split_a, 7 + n)
                rows = slice(n * FT // 2, (n + 1) * FT // 2)
                last = e.tensor_tensor(w2_lo[:, rows, :], w2_f[n], w2_hi[:, rows, :].bitcast(F32), ALU.subtract)
            last.then_inc(p_split_v, 1)
            e.wait_ge(p_pe, 1)
            e.tensor_tensor(bias_1[:, :], sc[0][:, 0:FT], bias_1in[:, :], ALU.add).then_inc(p_v, 1)
            e.wait_ge(p_pe, 2)
            e.tensor_tensor(bias_o[:, :], sc[1][:, 0:D], bias_o[:, :], ALU.add).then_inc(p_v, 1)
            e.wait_ge(p_v, 9)
            early(e, ht_l, sl, e_out, e_hn)
            run(e, ve_iteration)

        @block.tensor
        def _(e):
            e.wait_ge(p_const, 7)
            e.wait_ge(p_split_v, 5)
            e.wait_ge(p_dma, 16 * 8)
            for j in range(FT):
                for t in range(T):
                    last = e.matmul(sc[0][:, j:j + 1], w1_raw[t][:, j * P:(j + 1) * P], beta_c[:, t:t + 1],
                                    start=(t == 0), stop=(t == T - 1))
            last.then_inc(p_pe, 1)
            for t in range(T):
                last = e.matmul(sc[1][:, 0:D], bv_c[:, t:t + 1].to_broadcast([P, P]), stage_of("o")[:, t, :],
                                start=(t == 0), stop=(t == T - 1))
            last.then_inc(p_pe, 1)
            e.wait_ge(p_split_v, 7)
            e.wait_ge(p_v, 9)
            e.wait_ge(p_const, CONSTS)
            early(e, ht_pe, f_pe, z_pe)
            run(e, pe_iteration)


_INS = ["x", "wq_t", "bq", "wk_t", "bk", "wv_t", "bv", "wo_t", "bo", "gamma", "beta", "q1", "sc1", "b1", "q2", "sc2", "b2"]


def kernel(L0_attn_x, L0_attn_Wq, L0_attn_bq, L0_attn_Wk, L0_attn_bk, L0_attn_Wv, L0_attn_bv, L0_attn_Wo, L0_attn_bo,
           L0_ffn_ln_gamma, L0_ffn_ln_beta, L0_ffn_fc1_q, L0_ffn_fc1_scales, L0_ffn_fc1_bias,
           L0_ffn_fc2_q, L0_ffn_fc2_scales, L0_ffn_fc2_bias):
    import concourse.bacc as bacc
    from concourse.bass_utils import run_bass_kernel_spmd

    values = dict(zip(_INS, (
        L0_attn_x, np.asarray(L0_attn_Wq).T, L0_attn_bq, np.asarray(L0_attn_Wk).T, L0_attn_bk,
        np.asarray(L0_attn_Wv).T, L0_attn_bv, np.asarray(L0_attn_Wo).T, L0_attn_bo,
        L0_ffn_ln_gamma, L0_ffn_ln_beta, L0_ffn_fc1_q, L0_ffn_fc1_scales, L0_ffn_fc1_bias,
        L0_ffn_fc2_q, L0_ffn_fc2_scales, L0_ffn_fc2_bias)))
    nc = bacc.Bacc("TRN2", target_bir_lowering=False, num_devices=1)
    arrays, args = {}, []
    for name in _INS:
        a = np.ascontiguousarray(values[name])
        arrays[f"in_{name}"] = a
        args.append(nc.dram_tensor(f"in_{name}", a.shape, mybir.dt.from_np(a.dtype), kind="ExternalInput").ap())
    out = nc.dram_tensor("out", arrays["in_x"].shape, F32, kind="ExternalOutput").ap()
    build(nc, *args, out)
    r = run_bass_kernel_spmd(nc, [arrays], core_ids=[0])
    return r.results[0]["out"]
```

```python
from contextlib import ExitStack

import concourse.bass as bass
from concourse import mybir
import numpy as np

F32 = mybir.dt.float32
F32R = mybir.dt.float32r
I32 = mybir.dt.int32
ALU = mybir.AluOpType
ACT = mybir.ActivationFunctionType

P = 128
EPS = 1e-5


class Event:

    def __init__(self, sem, per, step=1, early=0):
        self.sem, self.per, self.step, self.early = sem, per, step, early

    def done(self, instruction):
        return instruction.then_inc(self.sem, self.step)

    def value(self, batch, k):
        return (batch + self.early) * (self.per * self.step) + (k + 1) * self.step


class Waiter:

    def __init__(self, engine, i):
        self.engine, self.i, self.known = engine, i, {}

    def alone(self, event, shift=0, k=None):
        self.need(event, shift, k)
        self.engine.sem_inc(self.idle, 1)

    def need(self, event, shift=0, k=None):
        k = event.per - 1 if k is None else k
        if self.known.get((id(event), shift), -1) >= k:
            return
        self.known[(id(event), shift)] = k
        value = event.value(self.i + shift, k)
        if not isinstance(value, int) or value > 0:
            self.engine.wait_ge(event.sem, value)


def build(nc, x, wq_t, bq, wk_t, bk, wv_t, bv, wo_t, bo, gamma, beta, q1, sc1, b1, q2, sc2, b2, out):
    B, S, D = x.shape
    F = q1.shape[1]
    HEADS = 16
    HD = D // HEADS
    C = S // P
    T = D // P
    HT = HEADS // T
    FT = F // P
    HALF = P // 2
    U = C * T
    HV = HT // 2
    G1, G2 = sc1.shape[0], sc2.shape[0]
    SLOTS = 4
    assert D == 2 * P and S == 4 * P and HD == 16 and G1 == T and G2 == FT

    x_v = x.rearrange("b (c p) d -> b p c d", p=P)
    out_v = out.rearrange("b (c p) d -> b p c d", p=P)

    with ExitStack() as ctx:
        def sb(name, shape, dtype=F32):
            return ctx.enter_context(nc.sbuf_tensor(name, shape, dtype))

        def bank(name):
            return ctx.enter_context(nc.psum_tensor(name, [P, 512], F32))

        def sem(name):
            return ctx.enter_context(nc.semaphore(name))

        w_hi = {n: sb(f"w{n}_hi", [P, T, D], F32R) for n in "qkvo"}
        w_lo = {n: sb(f"w{n}_lo", [P, T, D], F32R) for n in "qkvo"}
        w1_q = sb("w1_q", [P, T, F], F32R)
        w2_hi, w2_lo = sb("w2_hi", [P, FT, D], F32R), sb("w2_lo", [P, FT, D], F32R)
        ident = sb("ident", [P, P])
        head_ones = sb("head_ones", [P, P])
        head_ones_r = sb("head_ones_r", [P, P], F32R)
        causal = sb("causal", [P, P])
        head_col = sb("head_col", [P, HV])
        head_one = sb("head_one", [P, HT])
        ones = sb("ones", [P, 1])
        table_warm = sb("table_warm", [P, 1])
        minus_half = sb("minus_half", [P, C])
        bias_qk = sb("bias_qk", [P, 2, T])
        bias_qkm = sb("bias_qkm", [P, 2, T])
        bias_qk1 = sb("bias_qk1", [P, 2, T])
        scale_1 = sb("scale_1", [P, T, FT])
        bias_1 = sb("bias_1", [P, FT])
        beta_w1 = sb("beta_w1", [P, T, FT])
        bias_1in = sb("bias_1in", [P, FT])
        gamma_c, beta_c, bv_c = sb("gamma_c", [P, T]), sb("beta_c", [P, T]), sb("bv_c", [P, T])
        bias_o = sb("bias_o", [P, D])
        bias_2 = sb("bias_2", [P, D])

        x_in = sb("x_in", [P, C, D])
        xb = sb("xb", [P, C, D])
        x_hat = sb("x_hat", [P, C, D])
        xt_hi, xt_lo = sb("xt_hi", [P, T, S], F32R), sb("xt_lo", [P, T, S], F32R)
        clip = sb("clip", [P, 2, S])
        phi_q, phi_k = sb("phi_q", [P, T, S]), sb("phi_k", [P, T, S])
        qk = sb("qk", [P, T, S])
        qk_hi, qk_lo = xt_hi, xt_lo
        qh_hi, qh_lo = sb("qh_hi", [P, T, HV, S], F32R), sb("qh_lo", [P, T, HV, S], F32R)
        k_hi, k_lo = sb("k_hi", [P, T, S], F32R), sb("k_lo", [P, T, S], F32R)
        k_tok = sb("k_tok", [P, C, D])
        v_pad = sb("v_pad", [P, C, HT * T // 2, 4, HD])
        probs = [sb(f"probs{n}", [P, HT, P]) for n in range(2)]
        state = sb("state", [P, 2, T, P])
        gt_hi, gt_lo = sb("gt_hi", [P, T, S], F32R), sb("gt_lo", [P, T, S], F32R)
        x1 = sb("x1", [P, C, D])
        hn2 = sb("hn2", [P, C, D])
        res = sb("res", [P, C, D])
        silu_f = sb("silu_f", [P, SLOTS, S])
        s_hi, s_lo = sb("s_hi", [P, FT, S], F32R), sb("s_lo", [P, FT, S], F32R)
        stats1, stats2 = sb("stats1", [P, C, 6]), sb("stats2", [P, C, 6])
        mv1, mv2 = sb("mv1", [P, C, 2]), sb("mv2", [P, C, 2])
        ve1, rstd1 = sb("ve1", [P, C]), sb("rstd1", [P, C])
        tiny = sb("tiny", [P, 6, C])
        stage_qkvo = {n: t for n, t in zip("qkvo", (phi_q, phi_k, k_tok, x1))}
        half_w2 = [P, FT // 2, D]

        def staged(ap, shape=None):
            ap = ap.rearrange("p a n -> p (a n)")
            return ap if shape is None else ap.rearrange("p (g n) -> p g n", n=shape[-1])

        w1_i = [staged(probs[t][:, :, :]) for t in range(T)]
        w2_i = [v_pad[:, 2 * n:2 * n + 2, :, :, :].rearrange("p c r a x -> p (c r a x)").rearrange("p (g n) -> p g n", n=D)
                for n in range(2)]
        sc2_b = [staged(silu_f[:, 2 * n:2 * n + 2, :], half_w2) for n in range(2)]
        w2_f = [hn2, res]

        num = [bank(f"num{t}") for t in range(T)]
        state_acc = bank("state_acc")
        sc = [bank(f"sc{r}") for r in range(2)]
        ring = [bank(f"ring{n}") for n in range(3)]
        USES = ["v1", "ht0", "ht1", "f1a", "f1b", "den0", "f2a", "f2b", "den1", "f3a", "f3b", "f4a", "f4b",
                "f5a", "f5b", "f6a", "f6b", "f7a", "f7b", "xt0", "xt1", "k0", "q0", "z0", "z1", "wo0", "wo1"]
        NEXT_USES = {"xt0", "xt1", "k0", "q0"}
        BORROWED = {"v0": state_acc, "kt0": sc[0], "kt1": sc[1], "f0a": num[0], "f0b": num[1]}
        FFN_USES = {"ht0", "ht1", "z0", "z1"} | {f"f{j}{ab}" for j in range(FT) for ab in "ab"}

        def qk_bank(is_q, m):
            return num[is_q] if m else ring_bank("kq"[is_q] + "0")

        def ring_bank(use):
            return BORROWED[use] if use in BORROWED else ring[USES.index(use) % 3]

        def ev(name, per, **more):
            return Event(sem(name), per, **more)

        load = ev("load", 1, step=16)
        ln1_st = ev("ln1_st", 1)
        ln1_mv = ev("ln1_mv", 1)
        ln1_ve = ev("ln1_ve", 1)
        ln1_r = ev("ln1_r", 1)
        xhat = ev("xhat", 1)
        e_xb = ev("e_xb", 1)
        xt_pe, xt_h, xt_l = ev("xt_pe", T), ev("xt_h", T), ev("xt_l", T)
        qk_pe, qk_exp, qk_clip, phi = ev("qk_pe", 2 * T), ev("qk_exp", 2 * T), ev("qk_clip", 2 * T), ev("phi", 2 * T)
        v_pe, v_sb = ev("v_pe", C // 2), ev("v_sb", C)
        kt_pe, kt_sb = ev("kt_pe", C // 2), ev("kt_sb", C // 2)
        kcum, qkcum, e_qkh, e_qkl = ev("kcum", T), ev("qkcum", T), ev("e_qkh", T), ev("e_qkl", T)
        e_kh, e_kl, e_qh, e_ql = ev("e_kh", T), ev("e_kl", T), ev("e_qh", T), ev("e_ql", T)
        sc_pe = ev("sc_pe", U)
        POOL_MASKS = (2, 3, 4, 5)
        VE_MASKS = [range(U), [u for u in range(U) if u not in POOL_MASKS]]
        masked = [ev(f"masked{r}", len(VE_MASKS[r])) for r in range(2)]
        copied, po_masked = ev("copied", len(POOL_MASKS)), ev("po_masked", len(POOL_MASKS))

        def need_masked(w, u, r):
            if u in VE_MASKS[r]:
                w.need(masked[r], 0, VE_MASKS[r].index(u))
            else:
                w.need(po_masked, 0, POOL_MASKS.index(u))
        upd_pe, snap = ev("upd_pe", C - 1), ev("snap", C - 1)
        av_pe = ev("av_pe", U)
        den_pe, den_sb, rden = ev("den_pe", T), ev("den_sb", T), ev("rden", U)
        attn, at_h, at_l = ev("attn", T), ev("at_h", T), ev("at_l", T)
        wo_pe, e_x1 = ev("wo_pe", C // 2), ev("e_x1", C // 2)
        ln2_v = ev("ln2_v", 7)
        ln2_p = ev("ln2_p", 2)
        e_hn2 = ev("e_hn2", C)
        F_ = dict(early=1)
        e_hn, res_a, e_res = ev("e_hn", 1, **F_), ev("res_a", 1, **F_), ev("e_res", 1, **F_)
        ht_pe, ht_h, ht_l = ev("ht_pe", T, **F_), ev("ht_h", T, **F_), ev("ht_l", T, **F_)
        f_pe = ev("f_pe", T * FT, **F_)
        f_a, f_b = ev("f_a", FT, **F_), ev("f_b", FT, **F_)
        silu, sh, sl = ev("silu", FT, **F_), ev("sh", FT, **F_), ev("sl", FT, **F_)
        z_pe, e_out = ev("z_pe", C // 2, **F_), ev("e_out", C // 2, **F_)
        store = ev("store", 2, step=16, **F_)

        Waiter.idle = sem("idle")
        p_const, p_bias, p_dma = sem("p_const"), sem("p_bias"), sem("p_dma")
        p_wdma = {n: sem(f"p_wdma_{n}") for n in ("k", "q", "v", "o", "1", "2")}
        p_split_a, p_split_v, p_v, p_pe = sem("p_split_a"), sem("p_split_v"), sem("p_v"), sem("p_pe")

        LAST_READ = {
            "v1": (v_sb, 3), "ht0": (ht_l, 0), "ht1": (ht_l, 1), "den0": (den_sb, 0),
            "den1": (den_sb, 1), "z0": (e_out, 0), "z1": (e_out, 1), "wo0": (e_x1, 0), "wo1": (e_x1, 1),
            "xt0": (xt_l, 0), "xt1": (xt_l, 1), "k0": (phi, 0), "q0": (phi, 1),
        } | {f"f{j}{ab}": ((f_a, f_b)["ab".index(ab)], j) for j in range(FT) for ab in "ab"}

        def batch_shift(use):
            return -1 if use in FFN_USES else 1 if use in NEXT_USES else 0

        def free_bank(w, use, present):
            if use == "v0":
                w.need(snap, -1)
                return
            if use in ("kt0", "kt1"):
                w.need(masked[int(use[-1])], -1)
                return
            if use in ("f0a", "f0b"):
                w.need(*((phi, 0, 3) if "v1" in present else (attn, -1)))
                return
            n = USES.index(use)
            m = n - 1
            while True:
                earlier = m < 0
                other = USES[m % len(USES)]
                shift = batch_shift(other) - earlier
                exists = other in present or (earlier and not (isinstance(w.i, int) and w.i + shift >= B))
                if USES.index(other) % 3 == USES.index(use) % 3 and exists:
                    event, k = LAST_READ[other]
                    w.need(event, shift, k)
                    return
                m -= 1

        def pe_split3(e, target, pairs):
            n = 0
            for (lh, ll), (rh, rl) in pairs:
                for a, b in ((lh, rh), (lh, rl), (ll, rh)):
                    last = e.matmul(target, a, b, start=(n == 0), stop=(n == 3 * len(pairs) - 1))
                    n += 1
            return last

        def pe_projection(e, w, n, m, s, present):
            if m:
                w.need(attn, s - 1)
            else:
                free_bank(w, n + "0", present)
            cols = slice(m * P, (m + 1) * P)
            last = pe_split3(e, qk_bank("kq".index(n), m)[:, :], [
                ((w_hi[n][:, t, cols], w_lo[n][:, t, cols]), (xt_hi[:, t, :], xt_lo[:, t, :])) for t in range(T)])
            qk_pe.done(last)

        def pe_tokens(e, w, n, lhs, use, present, event):
            free_bank(w, use, present)
            for h in range(2):
                toks = slice((2 * int(use[-1]) + h) * P, (2 * int(use[-1]) + h + 1) * P)
                last = pe_split3(e, ring_bank(use)[:, h * D:(h + 1) * D], [
                    ((lhs[0][:, t, toks], lhs[1][:, t, toks]), (w_hi[n][:, t, :], w_lo[n][:, t, :])) for t in range(T)])
            event.done(last)

        def pe_transposes(e, w, src, t, use, present, event, chunk_ready=None):
            free_bank(w, use, present)
            for c in range(C):
                if chunk_ready:
                    chunk_ready(c)
                last = e.transpose(ring_bank(use)[:, c * P:(c + 1) * P], src[:, c, t * P:(t + 1) * P], ident[:, :])
            event.done(last)

        def pe_iteration(e, i, A, Fn, N):
            w = Waiter(e, i)
            present = {u for u in USES if (Fn if u in FFN_USES else N if u in NEXT_USES else A)}

            def x_transposes():
                w.need(xhat, 1)
                for t in range(T):
                    pe_transposes(e, w, x_hat, t, f"xt{t}", present, xt_pe)

            def ffn_in():
                for t in range(T):
                    pe_transposes(e, w, hn2, t, f"ht{t}", present, ht_pe, lambda c: w.need(e_hn2, -1, c))

            def fc1(j):
                if not Fn:
                    return
                w.need(ht_l, -1)
                cols = slice(j * P, (j + 1) * P)
                for t in range(T):
                    use = f"f{j}{'ab'[t]}"
                    free_bank(w, use, present)
                    e.matmul(ring_bank(use)[:, :], w1_q[:, t, cols], gt_hi[:, t, :], start=True, stop=False)
                    f_pe.done(e.matmul(ring_bank(use)[:, :], w1_q[:, t, cols], gt_lo[:, t, :], start=False, stop=True))

            def fc2(c):
                if not Fn:
                    return
                w.need(sh, -1)
                w.need(sl, -1)
                n, h = divmod(c, 2)
                if h == 0:
                    free_bank(w, f"z{n}", present)
                toks = slice(c * P, (c + 1) * P)
                last = pe_split3(e, ring_bank(f"z{n}")[:, h * D:(h + 1) * D], [
                    ((s_hi[:, j, toks], s_lo[:, j, toks]), (w2_hi[:, j, :], w2_lo[:, j, :])) for j in range(FT)])
                if h:
                    z_pe.done(last)

            def k_transposes(n):
                w.need(phi, 0, 2)
                free_bank(w, f"kt{n}", present)
                for h in range(2):
                    for t in range(T):
                        c = 2 * n + h
                        last = e.transpose(ring_bank(f"kt{n}")[:, (h * T + t) * P:(h * T + t + 1) * P],
                                           phi_k[:, t, c * P:(c + 1) * P], ident[:, :])
                kt_pe.done(last)

            def scores(u):
                c, t = divmod(u, T)
                w.need(e_kl, 0, t)
                if u == 0:
                    w.need(kt_sb, 0)
                toks = slice(c * P, (c + 1) * P)
                for n, (ks, qs) in enumerate(((k_hi, qh_hi), (k_lo, qh_hi), (k_hi, qh_lo))):
                    if n == 0:
                        w.need(e_qh, 0, t)
                    if n == 2:
                        w.need(e_ql, 0, t)
                    for r in range(2):
                        if r and u - 1 in POOL_MASKS:
                            w.need(copied, 0, POOL_MASKS.index(u - 1))
                        elif u:
                            need_masked(w, u - 1, r)
                        half = slice(r * HALF, (r + 1) * HALF)
                        last = e.matmul(sc[r][:, :], ks[half, t, toks], qs[half, t, :, toks],
                                        start=(n == 0), stop=(n == 2))
                sc_pe.done(last)

            def from_state(u):
                c, t = divmod(u, T)
                if c:
                    w.need(snap, 0, c - 1)
                    e.matmul(num[t][:, c * P:(c + 1) * P], state[:, (c - 1) % 2, t, :], phi_q[:, t, c * P:(c + 1) * P],
                             start=False, stop=False, skip_group_check=True)

            def update_state(c):
                w.need(kt_sb, 0, c // 2)
                w.need(v_sb, 0, max(c, 1))
                if c:
                    w.need(snap, 0, c - 1)
                for t in range(T):
                    last = e.matmul(state_acc[:, t * P:(t + 1) * P], k_tok[:, c, t * P:(t + 1) * P],
                                    v_pad[:, c, t * HT // 2:(t + 1) * HT // 2, 0:4:3, :],
                                    start=(c == 0 and t == 0), stop=True, skip_group_check=True)
                upd_pe.done(last)

            def values(u):
                c, t = divmod(u, T)
                for r in range(2):
                    need_masked(w, u, r)
                w.need(v_sb, 0, c)
                if c == 0:
                    w.need(phi, 0)
                    if Fn:
                        w.need(f_b, -1, 0)
                for odd in range(2):
                    for pair in range(HT // 2):
                        last = e.matmul(
                            num[t][32 * pair:32 * pair + 32, c * P:(c + 1) * P],
                            v_pad[:, c, t * HT // 2 + pair, 2 * odd:2 * odd + 2, :],
                            probs[u % 2][:, 2 * pair + odd, :],
                            start=(c == 0 and odd == 0), stop=(odd == 1), skip_group_check=True)
                av_pe.done(last)

            def denominator(t):
                w.need(e_qkl, 0, t)
                free_bank(w, f"den{t}", present)
                e.matmul(ring_bank(f"den{t}")[:, :], head_ones_r[:, :], qk_hi[:, t, :], start=True, stop=False)
                den_pe.done(e.matmul(ring_bank(f"den{t}")[:, :], head_ones_r[:, :], qk_lo[:, t, :], start=False, stop=True))

            def project_kq(m):
                if N:
                    w.need(xt_l, 1)
                    pe_projection(e, w, "k", m, 1, present)
                    pe_projection(e, w, "q", m, 1, present)

            def project_v(n):
                if A:
                    w.need(xt_l)
                    pe_tokens(e, w, "v", (xt_hi, xt_lo), f"v{n}", present, v_pe)

            project_v(0)
            if Fn:
                ffn_in()
            project_v(1)
            if A:
                k_transposes(0)
                k_transposes(1)
            fc1(0)
            fc1(1)
            if A:
                update_state(0)
                scores(0)
            fc1(2)
            if A:
                denominator(0)
            if A:
                scores(1)
                values(0)
                denominator(1)
            for u in range(2, U):
                if u < 7:
                    fc1(u + 1)
                if A:
                    if u % T == 0 and u // T < C - 1:
                        update_state(u // T)
                    scores(u)
                if u == 6 and N:
                    x_transposes()
                if A:
                    from_state(u - 1)
                    values(u - 1)
            project_kq(0)
            fc2(0)
            if A:
                from_state(U - 1)
                values(U - 1)
            fc2(1)
            if A:
                w.need(at_l)
                for n in range(2):
                    pe_tokens(e, w, "o", (gt_hi, gt_lo), f"wo{n}", present, wo_pe)
            project_kq(1)
            fc2(2)
            fc2(3)

        def half_probs(u, r):
            return probs[u % 2][:, r * HV:(r + 1) * HV, :]

        def mask_half(e, w, u, r):
            w.need(sc_pe, 0, u)
            if u >= 2:
                w.need(av_pe, 0, u - 2)
            else:
                w.need(av_pe, -1)
            masked[r].done(e.tensor_tensor(
                half_probs(u, r), sc[r][:, :].rearrange("p (h q) -> p h q", h=HV),
                causal[:, None, :].to_broadcast([P, HV, P]), ALU.mult))

        def ve_norm_x(e, w, s):
            w.need(load, s)
            for c in range(C):
                last = e.bn_stats(stats1[:, c, :], x_in[:, c, :])
            ln1_st.done(last)
            w.alone(ln1_st, s)
            for c in range(C):
                last = e.bn_aggr(mv1[:, c, :], stats1[:, c, :])
            ln1_mv.done(last)
            w.need(ln1_mv, s)
            ln1_ve.done(e.tensor_scalar(ve1[:, :], mv1[:, :, 1], EPS, None, ALU.add))

        def ve_x_hat(e, w, s, c):
            w.need(ln1_r, s)
            w.need(xt_pe, s - 1)
            last = e.tensor_scalar(x_hat[:, c, :], x_in[:, c, :], mv1[:, c, 0:1], rstd1[:, c:c + 1],
                                   ALU.subtract, ALU.mult)
            if c == C - 1:
                xhat.done(last)

        def ve_lo(e, w, bank_, hi, lo, t, hi_event, shift, event):
            w.need(hi_event, shift, t)
            event.done(e.tensor_tensor(lo[:, t, :], bank_, hi[:, t, :].bitcast(F32), ALU.subtract))

        def ve_iteration(e, i, A, Fn, N, preparation=(None, None, None)):
            w = Waiter(e, i)

            def features(n, s):
                m, is_q = n // 2, n % 2
                w.need(qk_exp, s, n)
                w.need(av_pe, s - 1, U - T + m)
                dst = phi_q if is_q else phi_k
                phi.done(e.scalar_tensor_tensor(
                    out=dst[:, m, :], in0=qk_bank(is_q, m)[:, :], scalar=bias_qk1[:, 1 - is_q, m:m + 1],
                    in1=clip[:, n % 2, :], op0=ALU.add, op1=ALU.max))

            def next_features(n):
                if N:
                    features(n, 1)

            def cumulate(t, s):
                w.need(phi, s, 2 * t)
                w.need(attn, s - 1)
                kcum.done(e.tensor_tensor_scan(qk[:, t, :], ones[:, 0:1].to_broadcast([P, S]), phi_k[:, t, :], 0.0,
                                               ALU.mult, ALU.add))

            def split_lo(t, s):
                w.need(sc_pe, s - 1, U - T + t)
                w.need(e_qh, s, t)
                for v in range(HV):
                    last = e.scalar_tensor_tensor(
                        out=qh_lo[:, t, v, :], in0=phi_q[:, t, :], scalar=head_col[:, v:v + 1],
                        in1=qh_hi[:, t, v, :].bitcast(F32), op0=ALU.mult, op1=ALU.subtract)
                e_ql.done(last)

            def ffn_sum(j):
                if not Fn:
                    return
                w.need(f_a, -1, j)
                w.need(f_pe, -1, T * j + 1)
                slot = silu_f[:, j % SLOTS, :]
                f_b.done(e.scalar_tensor_tensor(out=slot, in0=ring_bank(f"f{j}b")[:, :], scalar=scale_1[:, 1, j:j + 1],
                                                in1=slot, op0=ALU.mult, op1=ALU.add))

            def mask(u):
                for r in range(1 if u in POOL_MASKS else 2):
                    mask_half(e, w, u, r)

            def snapshot(c):
                w.need(upd_pe, 0, c)
                if c >= 2:
                    w.need(av_pe, 0, T * c - 1)
                else:
                    w.need(av_pe, -1)
                snap.done(e.tensor_tensor(state[:, c % 2, :, :], state_acc[:, 0:T * P].rearrange("p (t f) -> p t f", t=T),
                                          head_ones[:, None, :].to_broadcast([P, T, P]), ALU.mult))

            def reciprocals(t, n):
                w.need(den_sb, 0, t)
                part = qk[:, t, n * P:(n + 1) * P]
                rden.done(e.reciprocal(part, part))

            def final(n):
                w.need(z_pe, -1, n)
                w.need(e_res, -1)
                cs = slice(2 * n, 2 * n + 2)
                e_out.done(e.scalar_tensor_tensor(
                    out=res[:, cs, :], in0=ring_bank(f"z{n}")[:, :].rearrange("p (c d) -> p c d", c=2), scalar=0.5,
                    in1=res[:, cs, :], op0=ALU.mult, op1=ALU.add))

            if Fn:
                for t in range(T):
                    w.need(ht_h, -1, t)
                    ht_l.done(e.scalar_tensor_tensor(
                        out=gt_lo[:, t, :], in0=ring_bank(f"ht{t}")[:, :], scalar=gamma_c[:, t:t + 1],
                        in1=gt_hi[:, t, :].bitcast(F32), op0=ALU.mult, op1=ALU.subtract))
            if A:
                split_lo(1, 0)
            ffn_sum(0)
            ffn_sum(1)
            if A:
                mask(0)
                snapshot(0)
            if N:
                ve_norm_x(e, w, 1)
            if preparation[0]:
                preparation[0]()
            ffn_sum(2)
            if A:
                mask(1)
            if A:
                reciprocals(0, 0)
            for u in range(2, U):
                if u < 7:
                    ffn_sum(u + 1)
                if A:
                    mask(u)
                    if u % T == 0 and u // T < C - 1:
                        snapshot(u // T)
                    reciprocals(*divmod(u - 1, C))
                if N and 2 <= u < 2 + C:
                    ve_x_hat(e, w, 1, u - 2)
                if Fn and 2 <= u < 2 + C:
                    c = u - 2
                    w.need(store, -2)
                    last = e.tensor_scalar(res[:, c, :], x1[:, c, :], mv2[:, c, 0:1], tiny[:, 1, c:c + 1],
                                           ALU.subtract, ALU.mult)
                    if c == C - 1:
                        e_hn.done(last)
                if N and u == 6:
                    for t in range(T):
                        ve_lo(e, w, ring_bank(f"xt{t}")[:, :], xt_hi, xt_lo, t, xt_h, 1, xt_l)
            if A:
                reciprocals(T - 1, C - 1)

            def attention(t):
                w.need(rden)
                w.need(av_pe, 0, U - T + t)
                attn.done(e.tensor_tensor(qk[:, t, :], num[t][:, :], qk[:, t, :], ALU.mult))

            if A:
                attention(0)
            if preparation[1]:
                preparation[1]()
            next_features(0)
            next_features(1)
            if preparation[2]:
                preparation[2]()
            if A:
                ve_lo(e, w, qk[:, 0, :], gt_hi, gt_lo, 0, at_h, 0, at_l)
                attention(1)
                ve_lo(e, w, qk[:, 1, :], gt_hi, gt_lo, 1, at_h, 0, at_l)
            if Fn:
                final(0)
            if N:
                split_lo(0, 1)
                cumulate(0, 1)
            if A:
                w.need(e_xb)
                w.need(e_res, -1)
                for n in range(2):
                    w.need(wo_pe, 0, n)
                    cs = slice(2 * n, 2 * n + 2)
                    e_x1.done(e.tensor_tensor(x1[:, cs, :], ring_bank(f"wo{n}")[:, :].rearrange("p (c d) -> p c d", c=2),
                                              xb[:, cs, :], ALU.add))
                w.need(e_x1)
                for c in range(C):
                    last = e.bn_stats(stats2[:, c, :], x1[:, c, :])
                ln2_v.done(last)
                w.alone(ln2_v, 0, 0)
                for c in range(C):
                    last = e.bn_aggr(mv2[:, c, :], stats2[:, c, :])
                ln2_v.done(last)
                w.need(ln2_v, 0, 1)
                ln2_v.done(e.tensor_scalar(tiny[:, 0, :], mv2[:, :, 1], EPS, None, ALU.add))
                next_features(2)
                w.need(ln2_p, 0, 0)
                ln2_v.done(e.tensor_tensor(tiny[:, 2, :], tiny[:, 1, :], tiny[:, 1, :], ALU.mult))
                w.need(ln2_v, 0, 3)
                ln2_v.done(e.tensor_tensor(tiny[:, 2, :], tiny[:, 2, :], mv2[:, :, 1], ALU.mult))
                w.need(ln2_v, 0, 4)
                ln2_v.done(e.tensor_scalar(tiny[:, 3, :], tiny[:, 2, :], EPS, None, ALU.add))
                next_features(3)
                w.need(ln2_p, 0, 1)
                ln2_v.done(e.tensor_tensor(tiny[:, 5, :], tiny[:, 4, :], tiny[:, 1, :], ALU.mult))
                w.need(ln2_v)
                w.need(ht_pe, -1)
                for c in range(C):
                    e_hn2.done(e.tensor_scalar(hn2[:, c, :], x1[:, c, :], mv2[:, c, 0:1], tiny[:, 5, c:c + 1],
                                               ALU.subtract, ALU.mult))
            else:
                next_features(2)
                next_features(3)
            if Fn:
                final(1)
            if N:
                cumulate(1, 1)

        def ac_iteration(e, i, A, Fn, N):
            w = Waiter(e, i)

            def transposed_hi(use, t, pe_event, hi, shift, event):
                w.need(pe_event, shift, t)
                event.done(e.activation(hi[:, t, :], ring_bank(use)[:, :], ACT.Copy))

            def ffn_scaled(j):
                if not Fn:
                    return
                w.need(f_pe, -1, T * j)
                if j >= SLOTS:
                    w.need(sl, -1, j - SLOTS)
                else:
                    w.need(sl, -2)
                f_a.done(e.activation(silu_f[:, j % SLOTS, :], ring_bank(f"f{j}a")[:, :], ACT.Identity,
                                      bias=bias_1[:, j:j + 1], scale=scale_1[:, 0, j:j + 1]))

            def ffn_silu(j):
                if not Fn:
                    return
                slot = silu_f[:, j % SLOTS, :]
                w.need(f_b, -1, j)
                silu.done(e.activation(slot, slot, ACT.Silu))
                w.need(silu, -1, j)
                w.need(z_pe, -2)
                sh.done(e.activation(s_hi[:, j, :], slot, ACT.Copy))

            def k_split_hi(t, s):
                w.need(sc_pe, s - 1, U - T + t)
                w.need(phi, s, 2 * t)
                e_kh.done(e.activation(k_hi[:, t, :], phi_k[:, t, :], ACT.Copy))

            def q_split_hi(t, s, heads=range(HV)):
                w.need(phi, s, 2 * t + 1)
                for v in heads:
                    last = e.activation(qh_hi[:, t, v, :], phi_q[:, t, :], ACT.Copy, scale=head_col[:, v:v + 1])
                if v == HV - 1:
                    e_qh.done(last)

            def exponentials(t, s):
                for n in (2 * t, 2 * t + 1):
                    m, is_q = n // 2, n % 2
                    w.need(qk_pe, s, n)
                    if n >= 2:
                        w.need(phi, s, n - 2)
                    else:
                        w.need(phi, s - 1)
                    part = clip[:, n % 2, :]
                    qk_clip.done(e.activation(part, qk_bank(is_q, m)[:, :], ACT.Relu,
                                              bias=bias_qkm[:, 1 - is_q, m:m + 1], scale=-1.0))
                    w.need(qk_clip, s, n)
                    qk_exp.done(e.activation(part, part, ACT.Exp, scale=-1.0))

            def products_hi(t):
                if A:
                    w.need(qkcum, 0, t)
                    w.need(v_pe, 0)
                    e_qkh.done(e.activation(qk_hi[:, t, :], qk[:, t, :], ACT.Copy))

            if Fn:
                for t in range(T):
                    w.need(wo_pe, -1)
                    w.need(ht_pe, -1, t)
                    ht_h.done(e.activation(gt_hi[:, t, :], ring_bank(f"ht{t}")[:, :], ACT.Copy,
                                           scale=gamma_c[:, t:t + 1]))
            if A:
                for c in range(C):
                    w.need(v_pe, 0, c // 2)
                    if c == 0:
                        w.need(av_pe, -1)
                    h = c % 2
                    v_sb.done(e.activation(
                        v_pad[:, c, :, 0:4:3, :],
                        ring_bank(f"v{c // 2}")[:, h * D:(h + 1) * D].rearrange("p (r a x) -> p r a x", a=2, x=HD),
                        ACT.Copy))
            if A:
                for n in range(2):
                    w.need(kt_pe, 0, n)
                    w.need(upd_pe, -1)
                    kt_sb.done(e.activation(k_tok[:, 2 * n:2 * n + 2, :],
                                            ring_bank(f"kt{n}")[:, :].rearrange("p (c d) -> p c d", c=2), ACT.Copy))
            ffn_scaled(0)
            products_hi(0)
            ffn_scaled(1)
            products_hi(1)
            ffn_silu(0)
            if A:
                w.need(den_pe, 0, 0)
                den_sb.done(e.activation(qk[:, 0, :], ring_bank("den0")[:, :], ACT.Copy))
            ffn_scaled(2)
            ffn_silu(1)
            if A:
                w.need(den_pe, 0, 1)
                den_sb.done(e.activation(qk[:, 1, :], ring_bank("den1")[:, :], ACT.Copy))
            def copy_scores(u):
                if A and u in POOL_MASKS:
                    w.need(sc_pe, 0, u)
                    w.need(av_pe, 0, u - 2)
                    copied.done(e.activation(half_probs(u, 1), sc[1][:, :].rearrange("p (h q) -> p h q", h=HV), ACT.Copy))

            for j in range(3, FT - 1):
                ffn_scaled(j)
                copy_scores(j - 1)
                ffn_silu(j - 1)
            copy_scores(FT - 2)
            ffn_scaled(FT - 1)
            if N:
                for t in range(T):
                    w.need(den_pe, 0)
                    transposed_hi(f"xt{t}", t, xt_pe, xt_hi, 1, xt_h)
            ffn_silu(FT - 2)
            ffn_silu(FT - 1)
            if N:
                e.activation(table_warm[:, 0:1], ones[:, 0:1], ACT.Exp)
                exponentials(0, 1)

            def attention_hi(t):
                if A:
                    w.need(attn, 0, t)
                    w.need(f_pe, -1)
                    at_h.done(e.activation(gt_hi[:, t, :], qk[:, t, :], ACT.Copy))

            attention_hi(0)
            if N:
                k_split_hi(0, 1)
                q_split_hi(0, 1, range(HV // 2))
            attention_hi(1)
            if N:
                q_split_hi(0, 1, range(HV // 2, HV))
                exponentials(1, 1)
                k_split_hi(1, 1)
                q_split_hi(1, 1)

        def po_norm(e, w, s):
            w.need(ln1_ve, s)
            w.need(xhat, s - 1)
            ln1_r.done(e.tensor_tensor(rstd1[:, :], ve1[:, :], minus_half[:, :], ALU.pow))

        def po_xb(e, w, s):
            w.need(load, s)
            w.need(e_x1, s - 1)
            if isinstance(w.i, int) and w.i < 0:
                e.wait_ge(p_v, V_W2)
                e.memset(v_pad[:, :, :, :, :], 0.0).then_inc(p_const, 1)
                e.wait_ge(p_v, V_BIAS_O)
            e_xb.done(e.tensor_tensor(xb[:, :, :], x_in[:, :, :], bias_o[:, None, :].to_broadcast([P, C, D]), ALU.add))

        def po_iteration(e, i, A, Fn, N):
            w = Waiter(e, i)
            def ffn_lo(j):
                if not Fn:
                    return
                w.need(sh, -1, j)
                w.need(z_pe, -2)
                sl.done(e.tensor_tensor(s_lo[:, j, :], silu_f[:, j % SLOTS, :], s_hi[:, j, :].bitcast(F32), ALU.subtract))

            def products_lo(t):
                if A:
                    w.need(e_qkh, 0, t)
                    w.need(v_pe, 0)
                    e_qkl.done(e.tensor_tensor(qk_lo[:, t, :], qk[:, t, :], qk_hi[:, t, :].bitcast(F32), ALU.subtract))

            products_lo(0)
            products_lo(1)
            if N:
                po_norm(e, w, 1)
            ffn_lo(0)
            ffn_lo(1)
            for j in range(2, FT):
                if A and j in POOL_MASKS:
                    w.need(copied, 0, POOL_MASKS.index(j))
                    po_masked.done(e.tensor_tensor(half_probs(j, 1), half_probs(j, 1),
                                                   causal[:, None, :].to_broadcast([P, HV, P]), ALU.mult))
                ffn_lo(j)
            if Fn:
                w.need(e_hn, -1)
                res_a.done(e.tensor_tensor(res[:, :, :], x1[:, :, :], res[:, :, :], ALU.add))
                w.need(res_a, -1)
                e_res.done(e.tensor_tensor(res[:, :, :], res[:, :, :], bias_2[:, None, :].to_broadcast([P, C, D]), ALU.add))

            def split_lo(t, s):
                w.need(e_kh, s, t)
                w.need(sc_pe, s - 1, U - T + t)
                e_kl.done(e.tensor_tensor(k_lo[:, t, :], phi_k[:, t, :], k_hi[:, t, :].bitcast(F32), ALU.subtract))

            if N:
                split_lo(0, 1)
                po_xb(e, w, 1)
            if A:
                w.need(ln2_v, 0, 2)
                ln2_p.done(e.tensor_tensor(tiny[:, 1, :], tiny[:, 0, :], minus_half[:, :], ALU.pow))
                w.need(ln2_v, 0, 5)
                ln2_p.done(e.tensor_tensor(tiny[:, 4, :], tiny[:, 3, :], minus_half[:, :], ALU.pow))
            if N:
                for t in range(T):
                    w.need(kcum, 1, t)
                    w.need(phi, 1, 2 * t + 1)
                    qkcum.done(e.tensor_tensor(qk[:, t, :], qk[:, t, :], phi_q[:, t, :], ALU.mult))
                split_lo(1, 1)

        def sp_load(e, w, s, batch):
            w.need(xhat, s - 1)
            w.need(e_xb, s - 1)
            load.done(e.dma_start(x_in[:, :, :], x_v[batch]))

        def sp_iteration(e, i, A, Fn, N, N2):
            w = Waiter(e, i)
            for n in range(2):
                if Fn:
                    w.need(e_out, -1, n)
                    cs = slice(2 * n, 2 * n + 2)
                    store.done(e.dma_start(out_v[i - 1][:, cs, :], res[:, cs, :]))
                if N2 and n == 0:
                    sp_load(e, w, 2, i + 2)

        def run(e, iteration):
            iteration(e, 0, True, False, True)
            with e.Fori(1, B - 1) as i:
                iteration(e, i, True, True, True)
            iteration(e, B - 1, True, True, False)
            iteration(e, B, False, True, False)

        def early(e, *events):
            for v in events:
                e.sem_inc(v.sem, v.per * v.step)

        block = ctx.enter_context(nc.Block())

        WORDER = "kqvo"
        DMAS = 8
        V_W2, V_W1, V_BIAS_O, V_BIAS_2 = 3, 4, 5, 6
        CONSTS = 6 + 6 + 2 + 1

        def stage_of(n):
            return stage_qkvo[n][:, 0:T, 0:D]

        @block.sync
        def _(e):
            e.dma_start(x_in[:, :, :], x_v[0]).then_inc(load.sem, 16)
            src = {"q": wq_t, "k": wk_t, "v": wv_t, "o": wo_t}
            for n in WORDER:
                e.dma_start(stage_of(n), src[n].rearrange("(t p) n -> p t n", p=P)).then_inc(p_wdma[n], 16)
            for n in range(2):
                e.dma_start(w2_i[n].bitcast(I32), q2[n * F // 2:(n + 1) * F // 2, :].rearrange("(g p) n -> p g n", p=P))\
                    .then_inc(p_wdma["2"], 16)
                e.dma_start(sc2_b[n],
                            sc2[n * FT // 2:(n + 1) * FT // 2, :].rearrange("(a g) n -> a g n", a=1)
                            .to_broadcast([P, FT // 2, D])).then_inc(p_wdma["2"], 16)
            for t in range(T):
                e.dma_start(w1_i[t].bitcast(I32), q1[t * P:(t + 1) * P, :]).then_inc(p_wdma["1"], 16)
            early(e, store)
            w = Waiter(e, -1)
            sp_load(e, w, 2, 1)
            sp_iteration(e, 0, True, False, True, True)
            with e.Fori(1, B - 2) as i:
                sp_iteration(e, i, True, True, True, True)
            sp_iteration(e, B - 2, True, True, True, False)
            sp_iteration(e, B - 1, True, True, False, False)
            sp_iteration(e, B, False, True, False, False)
            e.wait_ge(store.sem, store.value(B - 1, 1))

        @block.scalar
        def _(e):
            with nc.allow_non_contiguous_dma("small bias vectors, a feature per partition"):
                for dst, src in ((bias_qk[:, 0, :], bq), (bias_qk[:, 1, :], bk)):
                    e.dma_start(dst, src.rearrange("(t p) -> p t", p=P)).then_inc(p_bias, 16)
                for dst, src in ((bv_c[:, :], bv), (beta_c[:, :], beta), (gamma_c[:, :], gamma), (bias_1in[:, :], b1),
                                 *((scale_1[:, t, :], sc1[t]) for t in range(T))):
                    e.dma_start(dst, src.rearrange("(t p) -> p t", p=P)).then_inc(p_dma, 16)
            e.dma_start(bias_o[:, :], bo.rearrange("(a d) -> a d", a=1).to_broadcast([P, D])).then_inc(p_dma, 16)
            e.dma_start(bias_2[:, :], b2.rearrange("(a d) -> a d", a=1).to_broadcast([P, D])).then_inc(p_dma, 16)
            for n in WORDER:
                e.wait_ge(p_wdma[n], 16)
                e.activation(w_hi[n][:, :, :], stage_of(n), ACT.Copy).then_inc(p_split_a, 1)
            early(e, ht_h, silu, sh, f_a)
            e.wait_ge(p_v, 2)
            ac_iteration(e, -1, False, False, True)
            e.wait_ge(p_const, CONSTS)
            e.wait_ge(p_v, V_W2)
            for n in range(2):
                e.activation(w2_hi[:, n * FT // 2:(n + 1) * FT // 2, :], w2_f[n][:, :, :], ACT.Copy)\
                    .then_inc(p_split_a, 1)
            run(e, ac_iteration)

        @block.gpsimd
        def _(e):
            for tile_, value in ((ident, 0.0), (head_ones, 1.0), (causal, 1.0), (head_one, 1.0)):
                e.memset(tile_[:], value).then_inc(p_const, 1)
            e.memset(ones[:, :], 1.0).then_inc(p_const, 1)
            e.memset(minus_half[:, :], -0.5).then_inc(p_const, 1)
            e.wait_ge(p_const, 6)
            n = 6

            def select(ap, compare, base, pattern, mult, fill):
                nonlocal n
                e.affine_select(out=ap, in_=ap, compare_op=compare, fill=fill, base=base, pattern=pattern,
                                channel_multiplier=mult).then_inc(p_const, 1)
                n += 1
                e.wait_ge(p_const, n)

            select(ident[:, :], ALU.not_equal, 0, [[-1, P]], 1, 1.0)
            blocks = head_ones[:, :].rearrange("p (h x) -> p h x", x=HD)
            select(blocks, ALU.is_ge, 0, [[-HD, HT], [0, HD]], 1, 0.0)
            select(blocks, ALU.is_ge, HD - 1, [[HD, HT], [0, HD]], -1, 0.0)
            select(head_one[:, :], ALU.is_ge, 0, [[-HD, HT]], 1, 0.0)
            select(head_one[:, :], ALU.is_ge, HD - 1, [[HD, HT]], -1, 0.0)
            select(causal[:, :], ALU.is_ge, 0, [[1, P]], -1, 0.0)
            e.tensor_copy(head_ones_r[:, :], head_ones[:, :]).then_inc(p_const, 1)
            e.tensor_tensor(head_col[:, :], head_one[:, 0:HV], head_one[:, HV:HT], ALU.add).then_inc(p_const, 1)
            early(e, res_a, e_res, sl)
            po_iteration(e, -1, False, False, True)
            run(e, po_iteration)


        @block.vector
        def _(e):
            def weights_lo(names):
                for n in names:
                    e.wait_ge(p_split_a, WORDER.index(n) + 1)
                    e.tensor_tensor(w_lo[n][:, :, :], stage_of(n), w_hi[n][:, :, :].bitcast(F32), ALU.subtract)\
                        .then_inc(p_split_v, 1)

            def projections():
                weights_lo("kq")
                e.wait_ge(p_bias, 16 * 2)
                e.tensor_scalar(bias_qk1[:, :, :], bias_qk[:, :, :], 1.0, None, ALU.add).then_inc(p_v, 1)
                e.tensor_scalar(bias_qkm[:, :, :], bias_qk[:, :, :], -1.0, None, ALU.mult).then_inc(p_v, 1)

            def ffn_weights():
                e.wait_ge(p_wdma["2"], 16 * 4)
                for n in range(2):
                    last = e.scalar_tensor_tensor(out=w2_f[n][:, :, :], in0=w2_i[n].bitcast(I32), scalar=-128.0,
                                                  in1=sc2_b[n], op0=ALU.add, op1=ALU.mult)
                last.then_inc(p_v, 1)
                e.wait_ge(p_wdma["1"], 16 * T)
                for t in range(T):
                    last = e.tensor_scalar(w1_q[:, t, :], w1_i[t].bitcast(I32), -128.0, None, ALU.add)
                last.then_inc(p_v, 1)

            early(e, ht_l, f_b, e_out, e_hn)
            ve_iteration(e, -1, False, False, True, (projections, lambda: weights_lo("vo"), ffn_weights))
            e.wait_ge(p_pe, 1)
            e.tensor_tensor(bias_o[:, :], sc[0][:, 0:D], bias_o[:, :], ALU.add).then_inc(p_v, 1)
            e.tensor_scalar(bias_2[:, :], bias_2[:, :], 0.5, None, ALU.mult).then_inc(p_v, 1)
            e.wait_ge(p_pe, 2)
            e.tensor_tensor(beta_w1[:, :, :], sc[1][:, 0:T * FT].rearrange("p (t j) -> p t j", t=T), scale_1[:, :, :],
                            ALU.mult).then_inc(p_v, 1)
            e.wait_ge(p_v, V_BIAS_2 + 1)
            e.tensor_tensor(beta_w1[:, 0, :], beta_w1[:, 0, :], beta_w1[:, 1, :], ALU.add).then_inc(p_v, 1)
            e.wait_ge(p_v, V_BIAS_2 + 2)
            e.tensor_tensor(bias_1[:, :], beta_w1[:, 0, :], bias_1in[:, :], ALU.add).then_inc(p_v, 1)
            for n in range(2):
                e.wait_ge(p_split_a, len(WORDER) + 1 + n)
                rows = slice(n * FT // 2, (n + 1) * FT // 2)
                last = e.tensor_tensor(w2_lo[:, rows, :], w2_f[n][:, :, :], w2_hi[:, rows, :].bitcast(F32), ALU.subtract)
            last.then_inc(p_split_v, 1)
            run(e, ve_iteration)

        @block.tensor
        def _(e):
            e.wait_ge(p_const, 7)
            early(e, ht_pe, f_pe, z_pe)
            e.wait_ge(p_split_v, 2)
            pe_iteration(e, -1, False, False, True)
            e.wait_ge(p_dma, 16 * DMAS)
            for t in range(T):
                last = e.matmul(sc[0][:, 0:D], bv_c[:, t:t + 1].to_broadcast([P, P]), stage_of("o")[:, t, :],
                                start=(t == 0), stop=(t == T - 1))
            last.then_inc(p_pe, 1)
            e.wait_ge(p_v, V_W1)
            for t in range(T):
                for j in range(FT):
                    last = e.matmul(sc[1][:, t * FT + j:t * FT + j + 1], w1_q[:, t, j * P:(j + 1) * P].bitcast(F32),
                                    beta_c[:, t:t + 1], start=True, stop=True)
            last.then_inc(p_pe, 1)
            e.wait_ge(p_v, V_BIAS_2 + 1)
            e.wait_ge(p_split_v, len(WORDER))
            run(e, pe_iteration)


_INS = ["x", "wq_t", "bq", "wk_t", "bk", "wv_t", "bv", "wo_t", "bo", "gamma", "beta", "q1", "sc1", "b1", "q2", "sc2", "b2"]


def kernel(L0_attn_x, L0_attn_Wq, L0_attn_bq, L0_attn_Wk, L0_attn_bk, L0_attn_Wv, L0_attn_bv, L0_attn_Wo, L0_attn_bo,
           L0_ffn_ln_gamma, L0_ffn_ln_beta, L0_ffn_fc1_q, L0_ffn_fc1_scales, L0_ffn_fc1_bias,
           L0_ffn_fc2_q, L0_ffn_fc2_scales, L0_ffn_fc2_bias):
    import concourse.bacc as bacc
    from concourse.bass_utils import run_bass_kernel_spmd

    values = dict(zip(_INS, (
        L0_attn_x, np.asarray(L0_attn_Wq).T, L0_attn_bq, np.asarray(L0_attn_Wk).T, L0_attn_bk,
        np.asarray(L0_attn_Wv).T, L0_attn_bv, np.asarray(L0_attn_Wo).T, L0_attn_bo,
        L0_ffn_ln_gamma, L0_ffn_ln_beta, L0_ffn_fc1_q, L0_ffn_fc1_scales, L0_ffn_fc1_bias,
        L0_ffn_fc2_q, L0_ffn_fc2_scales, L0_ffn_fc2_bias)))
    nc = bacc.Bacc("TRN2", target_bir_lowering=False, num_devices=1)
    arrays, args = {}, []
    for name in _INS:
        a = np.ascontiguousarray(values[name])
        arrays[f"in_{name}"] = a
        args.append(nc.dram_tensor(f"in_{name}", a.shape, mybir.dt.from_np(a.dtype), kind="ExternalInput").ap())
    out = nc.dram_tensor("out", arrays["in_x"].shape, F32, kind="ExternalOutput").ap()
    build(nc, *args, out)
    r = run_bass_kernel_spmd(nc, [arrays], core_ids=[0])
    return r.results[0]["out"]
```
